# Optimizing a Trainium2 kernel written in Bass

```python
import numpy as np
import jax
import jax.numpy as jnp

def _softmax(x, axis=-1):
    return jax.nn.softmax(x, axis=axis)

def _gelu(x):
    return jax.nn.gelu(x, approximate=True)

def _silu(x):
    return jax.nn.silu(x)

def _sigmoid(x):
    return jax.nn.sigmoid(x)

def _layernorm(x, axis=-1, eps=1e-05):
    m = jnp.mean(x, axis=axis, keepdims=True)
    v = jnp.var(x, axis=axis, keepdims=True)
    return (x - m) / jnp.sqrt(v + eps)

def _scatter_add(tgt, idx, src, axis=0):
    return tgt.at[idx].add(src)

def _segment_sum(src, seg, n):
    return jax.ops.segment_sum(src, seg, n)
kernel_name = 'mk_vit_tower_d2_tok_img512_r4_68f498'

def setup_inputs(seed: int=0):
    np.random.seed(seed)
    _w = jnp.asarray

    def _rec_inputs():
        import jax
        import jax.numpy as jnp
        _rk = jax.random.key(seed)
        x = -0.000222058 + 0.999998 * jax.random.normal(jax.random.fold_in(_rk, 1), (64, 3, 64, 64), jnp.float32)
        return x
    x = _rec_inputs()

    def _L0_tok_setup():
        import jax, jax.numpy as jnp
        import numpy as np
        IMG, P, C, D = (64, 16, 3, 128)
        NP = (IMG // P) ** 2
        PD = P * P * C
        key = jax.random.key(seed)
        k1, k2, k3 = jax.random.split(key, 3)
        x = jax.random.normal(k1, (128, C, IMG, IMG), dtype=jnp.float32)
        W = jax.random.normal(k2, (D, PD), dtype=jnp.float32) * (1.0 / np.sqrt(PD))
        b = jax.random.normal(k3, (D,), dtype=jnp.float32) * 0.01
        return {'x': x, 'W': W, 'b': b}
    _L0_tok_all = _L0_tok_setup()
    _L0_tok_in = {k: v for k, v in _L0_tok_all.items() if k in ('W', 'b')}
    del _L0_tok_all

    def _L0_attn_setup():
        import jax, jax.numpy as jnp
        import numpy as np

        def _log_g(x):
            return jnp.where(x >= 0, jnp.log(jax.nn.relu(x) + 0.5), -jax.nn.softplus(-x))
        key = jax.random.key(seed)
        k1, k2, k3 = jax.random.split(key, 3)
        B, L, D, H = (4, 2048, 128, 256)
        x = jax.random.normal(k1, (B, L, D), dtype=jnp.float32)
        W_in = jax.random.normal(k2, (2 * H, D), dtype=jnp.float32) * 0.05
        b_in = jnp.zeros((2 * H,), dtype=jnp.float32)
        W_out = jax.random.normal(k3, (D, H), dtype=jnp.float32) * 0.05
        b_out = jnp.zeros((D,), dtype=jnp.float32)
        return {'x': x, 'W_in': W_in, 'b_in': b_in, 'W_out': W_out, 'b_out': b_out}
    _L0_attn_all = _L0_attn_setup()
    _L0_attn_in = {k: v for k, v in _L0_attn_all.items() if k in ('W_in', 'b_in', 'W_out', 'b_out')}
    del _L0_attn_all

    def _L0_ffn_setup():
        import jax, jax.numpy as jnp
        import numpy as np
        EPS = 1e-05
        TOP_K = 2

        def _moe_forward(x, Wg, W1, b1, W2, b2, gamma, beta):
            B, S, D = x.shape
            xf = x.reshape(-1, D)
            logits = xf @ Wg
            topv, topi = jax.lax.top_k(logits, TOP_K)
            gate_w = jax.nn.softmax(topv, axis=-1)
            h = jax.nn.relu(jnp.einsum('td,edh->teh', xf, W1) + b1[None])
            y = jnp.einsum('teh,ehd->ted', h, W2) + b2[None]
            mu = jnp.mean(y, axis=-1, keepdims=True)
            var = jnp.mean((y - mu) ** 2, axis=-1, keepdims=True)
            y = (y - mu) / jnp.sqrt(var + EPS) * gamma[None] + beta[None]
            y_sel = jnp.take_along_axis(y, topi[:, :, None], axis=1)
            out = jnp.sum(gate_w[:, :, None] * y_sel, axis=1)
            return out.reshape(B, S, D)
        key = jax.random.key(seed)
        ks = jax.random.split(key, 8)
        B, S, D, H, E = (4, 512, 128, 128, 8)
        sd = lambda fan_in: 1.0 / np.sqrt(fan_in)
        x = jax.random.normal(ks[0], (B, S, D), dtype=jnp.float32)
        Wg = jax.random.uniform(ks[1], (D, E), jnp.float32, -sd(D), sd(D))
        W1 = jax.random.uniform(ks[2], (E, D, H), jnp.float32, -sd(D), sd(D))
        b1 = jax.random.uniform(ks[3], (E, H), jnp.float32, -sd(D), sd(D))
        W2 = jax.random.uniform(ks[4], (E, H, D), jnp.float32, -sd(H), sd(H))
        b2 = jax.random.uniform(ks[5], (E, D), jnp.float32, -sd(H), sd(H))
        gamma = jnp.ones((E, D), jnp.float32)
        beta = jnp.zeros((E, D), jnp.float32)
        return {'x': x, 'Wg': Wg, 'W1': W1, 'b1': b1, 'W2': W2, 'b2': b2, 'gamma': gamma, 'beta': beta}
    _L0_ffn_all = _L0_ffn_setup()
    _L0_ffn_in = {k: v for k, v in _L0_ffn_all.items() if k in ('Wg', 'W1', 'b1', 'W2', 'b2', 'gamma', 'beta')}
    del _L0_ffn_all

    def _L1_attn_setup():
        import jax, jax.numpy as jnp
        import numpy as np
        import math
        D_MODEL = 128
        NUM_HEADS = 8
        B, S = (4, 256)
        key = jax.random.key(seed)
        ks = jax.random.split(key, 9)
        s = 1.0 / math.sqrt(D_MODEL)
        return {'x': jax.random.normal(ks[0], (B, S, D_MODEL), dtype=jnp.float32), 'Wq': jax.random.normal(ks[1], (NUM_HEADS, D_MODEL, D_MODEL), dtype=jnp.float32) * s, 'bq': jax.random.normal(ks[2], (NUM_HEADS, D_MODEL), dtype=jnp.float32) * s, 'Wk': jax.random.normal(ks[3], (NUM_HEADS, D_MODEL, D_MODEL), dtype=jnp.float32) * s, 'bk': jax.random.normal(ks[4], (NUM_HEADS, D_MODEL), dtype=jnp.float32) * s, 'Wv': jax.random.normal(ks[5], (NUM_HEADS, D_MODEL, D_MODEL), dtype=jnp.float32) * s, 'bv': jax.random.normal(ks[6], (NUM_HEADS, D_MODEL), dtype=jnp.float32) * s, 'Wo': jax.random.normal(ks[7], (NUM_HEADS * D_MODEL, D_MODEL), dtype=jnp.float32) * (1.0 / math.sqrt(NUM_HEADS * D_MODEL))}
    _L1_attn_all = _L1_attn_setup()
    _L1_attn_in = {k: v for k, v in _L1_attn_all.items() if k in ('Wq', 'bq', 'Wk', 'bk', 'Wv', 'bv', 'Wo')}
    del _L1_attn_all

    def _L1_ffn_setup():
        import jax, jax.numpy as jnp
        import numpy as np
        DIM = 128
        HID = 256
        E = 8
        K = 2
        B, S = (4, 512)
        key = jax.random.key(seed)
        ks = jax.random.split(key, 10)
        sd = DIM ** (-0.5)
        sh = HID ** (-0.5)
        return {'x': jax.random.normal(ks[0], (B, S, DIM), dtype=jnp.float32), 'gate_w': jax.random.normal(ks[1], (E, DIM), dtype=jnp.float32) * sd, 'biases': jnp.zeros((E,), dtype=jnp.float32), 'w1': jax.random.normal(ks[2], (E, DIM, HID), dtype=jnp.float32) * sd, 'w3': jax.random.normal(ks[3], (E, DIM, HID), dtype=jnp.float32) * sd, 'w2': jax.random.normal(ks[4], (E, HID, DIM), dtype=jnp.float32) * sh, 'sw1': jax.random.normal(ks[5], (DIM, HID), dtype=jnp.float32) * sd, 'sw3': jax.random.normal(ks[6], (DIM, HID), dtype=jnp.float32) * sd, 'sw2': jax.random.normal(ks[7], (HID, DIM), dtype=jnp.float32) * sh}
    _L1_ffn_all = _L1_ffn_setup()
    _L1_ffn_in = {k: v for k, v in _L1_ffn_all.items() if k in ('gate_w', 'biases', 'w1', 'w3', 'w2', 'sw1', 'sw3', 'sw2')}
    del _L1_ffn_all
    return {'x': x, 'L0_tok_W': _L0_tok_in['W'], 'L0_tok_b': _L0_tok_in['b'], 'L0_attn_W_in': _L0_attn_in['W_in'], 'L0_attn_b_in': _L0_attn_in['b_in'], 'L0_attn_W_out': _L0_attn_in['W_out'], 'L0_attn_b_out': _L0_attn_in['b_out'], 'L0_ffn_Wg': _L0_ffn_in['Wg'], 'L0_ffn_W1': _L0_ffn_in['W1'], 'L0_ffn_b1': _L0_ffn_in['b1'], 'L0_ffn_W2': _L0_ffn_in['W2'], 'L0_ffn_b2': _L0_ffn_in['b2'], 'L0_ffn_gamma': _L0_ffn_in['gamma'], 'L0_ffn_beta': _L0_ffn_in['beta'], 'L1_attn_Wq': _L1_attn_in['Wq'], 'L1_attn_bq': _L1_attn_in['bq'], 'L1_attn_Wk': _L1_attn_in['Wk'], 'L1_attn_bk': _L1_attn_in['bk'], 'L1_attn_Wv': _L1_attn_in['Wv'], 'L1_attn_bv': _L1_attn_in['bv'], 'L1_attn_Wo': _L1_attn_in['Wo'], 'L1_ffn_gate_w': _L1_ffn_in['gate_w'], 'L1_ffn_biases': _L1_ffn_in['biases'], 'L1_ffn_w1': _L1_ffn_in['w1'], 'L1_ffn_w3': _L1_ffn_in['w3'], 'L1_ffn_w2': _L1_ffn_in['w2'], 'L1_ffn_sw1': _L1_ffn_in['sw1'], 'L1_ffn_sw3': _L1_ffn_in['sw3'], 'L1_ffn_sw2': _L1_ffn_in['sw2']}

def reference(x, L0_tok_W, L0_tok_b, L0_attn_W_in, L0_attn_b_in, L0_attn_W_out, L0_attn_b_out, L0_ffn_Wg, L0_ffn_W1, L0_ffn_b1, L0_ffn_W2, L0_ffn_b2, L0_ffn_gamma, L0_ffn_beta, L1_attn_Wq, L1_attn_bq, L1_attn_Wk, L1_attn_bk, L1_attn_Wv, L1_attn_bv, L1_attn_Wo, L1_ffn_gate_w, L1_ffn_biases, L1_ffn_w1, L1_ffn_w3, L1_ffn_w2, L1_ffn_sw1, L1_ffn_sw3, L1_ffn_sw2):
    import jax
    import jax.numpy as jnp

    def _L0_tok_ref(x, W, b):
        import jax, jax.numpy as jnp
        import numpy as np
        IMG, P, C, D = (64, 16, 3, 128)
        NP = (IMG // P) ** 2
        PD = P * P * C
        B, c, H, Wd = x.shape
        xp = x.reshape(B, c, H // P, P, Wd // P, P)
        xp = xp.transpose(0, 2, 4, 1, 3, 5).reshape(B, NP, c * P * P)
        return jnp.einsum('bnk,dk->bnd', xp, W) + b

    def _L0_attn_ref(x, W_in, b_in, W_out, b_out):
        import jax, jax.numpy as jnp
        import numpy as np

        def _log_g(x):
            return jnp.where(x >= 0, jnp.log(jax.nn.relu(x) + 0.5), -jax.nn.softplus(-x))
        hg = jnp.einsum('bld,ed->ble', x, W_in) + b_in
        H = hg.shape[-1] // 2
        hidden, gate = (hg[..., :H], hg[..., H:])
        log_coeffs = -jax.nn.softplus(gate)
        log_z = -jax.nn.softplus(-gate)
        log_tilde_h = _log_g(hidden)
        a_star = jnp.cumsum(log_coeffs, axis=1)
        log_h = a_star + jax.lax.cumlogsumexp(log_z + log_tilde_h - a_star, axis=1)
        h = jnp.exp(log_h)
        out = jnp.einsum('blh,dh->bld', h, W_out) + b_out
        return out

    def _L0_ffn_ref(x, Wg, W1, b1, W2, b2, gamma, beta):
        import jax, jax.numpy as jnp
        import numpy as np
        EPS = 1e-05
        TOP_K = 2

        def _moe_forward(x, Wg, W1, b1, W2, b2, gamma, beta):
            B, S, D = x.shape
            xf = x.reshape(-1, D)
            logits = xf @ Wg
            topv, topi = jax.lax.top_k(logits, TOP_K)
            gate_w = jax.nn.softmax(topv, axis=-1)
            h = jax.nn.relu(jnp.einsum('td,edh->teh', xf, W1) + b1[None])
            y = jnp.einsum('teh,ehd->ted', h, W2) + b2[None]
            mu = jnp.mean(y, axis=-1, keepdims=True)
            var = jnp.mean((y - mu) ** 2, axis=-1, keepdims=True)
            y = (y - mu) / jnp.sqrt(var + EPS) * gamma[None] + beta[None]
            y_sel = jnp.take_along_axis(y, topi[:, :, None], axis=1)
            out = jnp.sum(gate_w[:, :, None] * y_sel, axis=1)
            return out.reshape(B, S, D)
        return _moe_forward(x, Wg, W1, b1, W2, b2, gamma, beta)

    def _L1_attn_ref(x, Wq, bq, Wk, bk, Wv, bv, Wo):
        import jax, jax.numpy as jnp
        import numpy as np
        import math
        D_MODEL = 128
        NUM_HEADS = 8
        B, S = (4, 256)
        q = jnp.einsum('bsd,hde->bhse', x, Wq) + bq[None, :, None, :]
        k = jnp.einsum('bsd,hde->bhse', x, Wk) + bk[None, :, None, :]
        v = jnp.einsum('bsd,hde->bhse', x, Wv) + bv[None, :, None, :]
        scores = jnp.einsum('bhqe,bhke->bhqk', q, k) / math.sqrt(D_MODEL)
        attn = jax.nn.softmax(scores, axis=-1)
        heads = jnp.einsum('bhqk,bhke->bhqe', attn, v)
        concat = heads.transpose(0, 2, 1, 3).reshape(heads.shape[0], heads.shape[2], -1)
        return concat @ Wo

    def _L1_ffn_ref(x, gate_w, biases, w1, w3, w2, sw1, sw3, sw2):
        import jax, jax.numpy as jnp
        import numpy as np
        DIM = 128
        HID = 256
        E = 8
        K = 2
        B, S = (4, 512)
        Bb, Ss, D = x.shape
        xt = x.reshape(Bb * Ss, D)
        shared = jax.nn.silu(xt @ sw1) * (xt @ sw3) @ sw2
        scores = xt @ gate_w.T
        _, idx = jax.lax.top_k(scores + biases, K)
        topv, _ = jax.lax.top_k(scores, K)
        p = jax.nn.sigmoid(topv)
        p = p / jnp.sum(p, axis=-1, keepdims=True)
        h = jax.nn.silu(jnp.einsum('td,edh->eth', xt, w1)) * jnp.einsum('td,edh->eth', xt, w3)
        y = jnp.einsum('eth,ehd->etd', h, w2)
        onehot = jax.nn.one_hot(idx, E, dtype=xt.dtype)
        comb = jnp.einsum('tk,tke->te', p, onehot)
        out = jnp.einsum('te,etd->td', comb, y) + shared
        return out.reshape(Bb, Ss, D)
    h = _L0_tok_ref(x, L0_tok_W, L0_tok_b)
    h = h + _L0_attn_ref(_layernorm(h, axis=-1), L0_attn_W_in, L0_attn_b_in, L0_attn_W_out, L0_attn_b_out)
    h = h + _L0_ffn_ref(_layernorm(h, axis=-1), L0_ffn_Wg, L0_ffn_W1, L0_ffn_b1, L0_ffn_W2, L0_ffn_b2, L0_ffn_gamma, L0_ffn_beta)
    h = h + _L1_attn_ref(_layernorm(h, axis=-1), L1_attn_Wq, L1_attn_bq, L1_attn_Wk, L1_attn_bk, L1_attn_Wv, L1_attn_bv, L1_attn_Wo)
    h = h + _L1_ffn_ref(_layernorm(h, axis=-1), L1_ffn_gate_w, L1_ffn_biases, L1_ffn_w1, L1_ffn_w3, L1_ffn_w2, L1_ffn_sw1, L1_ffn_sw3, L1_ffn_sw2)
    return h

_drawn_inputs = setup_inputs


def setup_inputs(seed=0):
    import zlib

    import numpy as np

    out = dict(_drawn_inputs(seed))
    spreads = {'L0_attn_b_in': (0.0, 0.1),
     'L0_attn_b_out': (0.0, 0.1),
     'L0_ffn_gamma': (1.0, 0.2),
     'L0_ffn_beta': (0.0, 0.1),
     'L1_ffn_biases': (0.0, 0.1)}
    factors = {}
    for name, (base, spread) in spreads.items():
        noise = np.random.default_rng([zlib.crc32(name.encode()), seed]).standard_normal(out[name].shape)
        drawn = base * np.exp(spread * noise) if base else spread * noise
        out[name] = jnp.asarray(drawn.astype(out[name].dtype))
    for name, factor in factors.items():
        out[name] = (out[name] * factor).astype(out[name].dtype)
    return out
```

```python
import concourse.bass as bass
from concourse import mybir
from contextlib import ExitStack

ALU = mybir.AluOpType
ACT = mybir.ActivationFunctionType
AX = mybir.AxisListType
F32 = mybir.dt.float32
F32R = mybir.dt.float32r
U32 = mybir.dt.uint32
I32 = mybir.dt.int32

P = 128
D = 128
TOK = 1024
NT = TOK // P
HALVES = 2
HT = NT // HALVES
HC = HT * P
SEQ = 16
KC = 6
HG = 2
E0 = 8
E1 = 9
NH = 8
EPS = 1e-5
SCALE = float(D) ** -0.5
MASKED = -1e30
BLK = 32


def build(nc, t, out):
    with ExitStack() as ctx:
        def sb(name, shape, dt=F32):
            return ctx.enter_context(nc.sbuf_tensor(name, shape, dt))

        def sem(name):
            return ctx.enter_context(nc.semaphore(name))

        bank = [ctx.enter_context(nc.psum_tensor(f"bank{i}", [P, 512], F32)) for i in range(8)]

        x_in = sb("x_in", [P, NT, KC, P])
        x_place = x_in[:, :, :, :].rearrange("p i c k -> p (i c k)")
        tok_w = sb("tok_w", [P, KC, D])
        tok_b = sb("tok_b", [P, D])
        gru_w = sb("gru_w", [P, 4 * P])
        gru_b = sb("gru_b", [P, 4])
        gru_wo = sb("gru_wo", [P, HG, D])
        gru_bo = sb("gru_bo", [P, D])
        att_w = sb("att_w", [P, 4, NH, D])
        wqT, wkT, wvT, wo = (att_w[:, i] for i in range(4))
        att_b = sb("att_b", [P, 3, NH])
        m0_gate = sb("m0_gate", [P, E0])
        m0_w1 = sb("m0_w1", [P, E0, P])
        m0_b1 = sb("m0_b1", [P, E0])
        m0_w2 = sb("m0_w2", [P, E0, D])
        m0_b2 = sb("m0_b2", [E0, D])
        m0_gamma = sb("m0_gamma", [P, E0, D])
        m0_beta = sb("m0_beta", [E0, D])
        m1_gate = sb("m1_gate", [P, E0])
        m1_bias = sb("m1_bias", [P, E0])
        m1_w13 = sb("m1_w13", [P, E1, 4, P])
        m1_w2 = sb("m1_w2", [P, E1, 2, D])

        ident = sb("ident", [P, P])
        ones = sb("ones", [P, P])
        ones8r = sb("ones8r", [E0, P], F32R)
        expo = sb("expo", [P, HT])
        block = sb("block", [P, NT, SEQ])
        mask = sb("mask", [P, 2 * NH, BLK])
        iota_i = sb("iota_i", [P, HT, E0], I32)
        iota8 = sb("iota8", [P, HT, E0])
        eps_c = sb("eps_c", [P, 1])
        zero = sb("zero", [P, 1])

        gruH = sb("gruH", [P, 4 * P], F32R)
        gruL = sb("gruL", [P, 4 * P], F32R)
        gru_bn = sb("gru_bn", [P, HG])
        gru_bh = sb("gru_bh", [P, HG])
        GH = sb("GH", [P, NH, D], F32R)
        GL = sb("GL", [P, NH, D], F32R)
        UH = sb("UH", [P, NH, D], F32R)
        UL = sb("UL", [P, NH, D], F32R)
        bqk = sb("bqk", [P, NH])
        att_small = sb("att_small", [P, 3 * NH])
        att_ob = sb("att_ob", [P, D])
        w1H = sb("w1H", [P, 2, P], F32R)
        w1L = sb("w1L", [P, 2, P], F32R)
        w2_mean = sb("w2_mean", [P, E0])
        w2c = sb("w2c", [P, E0, D])
        b2_mean = sb("b2_mean", [E0, 1])
        b2c = sb("b2c", [E0, D])
        b2x = sb("b2x", [E0, E0, D])
        b2xH = sb("b2xH", [E0, E0, D], F32R)
        b2xL = sb("b2xL", [E0, E0, D], F32R)
        w13H = sb("w13H", [P, 3, 4, P], F32R)
        w13L = sb("w13L", [P, 3, 4, P], F32R)

        h = sb("h", [P, NT, D])
        hb = sb("hb", [P, NT, D])
        stats = sb("stats", [P, NT, 6])
        mv = sb("mv", [P, NT, 2])
        ve = sb("ve", [P, NT])
        rstd = sb("rstd", [P, NT])
        xn = sb("xn", [P, HALVES, HT, D])
        xT = sb("xT", [P, TOK])
        xH = sb("xH", [P, TOK], F32R)
        xL = sb("xL", [P, TOK], F32R)
        gru = sb("gru", [P, 4 * HG, HC])
        gf = gru[:, 0:HG]
        gz = gru[:, HG:2 * HG]
        gs = gru[:, 2 * HG:3 * HG]
        gh = gru[:, 3 * HG:4 * HG]
        qT = att_w[:, :, :, :].rearrange("p a n d -> p (a n d)").rearrange("p (n c) -> p n c", c=HC)
        V = x_place[:, 0:HT * NH * D].rearrange("p (i n d) -> p i n d", n=NH, d=D)
        rr = sb("rr", [P, HT, NH])
        sT = sb("sT", [P, 2 * NH, BLK])
        sq_ = sb("sq_", [P, 2, 2 * NH, BLK])
        row = sb("row", [P, 4, 2 * NH])
        PX = x_place[:, 8 * HC:12 * HC].rearrange("p (a n q) -> p a n q", a=2, q=P)
        lg = sb("lg", [P, HT, E0])
        lgb = sb("lgb", [P, HT, E0])
        top = sb("top", [P, HT, 8])
        topb = sb("topb", [P, HT, 8])
        idx = sb("idx", [P, HT, 8], U32)
        idf = sb("idf", [P, HT, 2])
        gw2 = sb("gw2", [P, HT, 2])
        gwt = sb("gwt", [P, HT, 2])
        eq = sb("eq", [P, HT, E0])
        comb0 = sb("comb0", [P, E0, NT])
        comb1 = sb("comb1", [P, E1, NT])
        combt = sb("combt", [P, NT, E0])
        gT = sb("gT", [E0, HC])
        hid0 = x_place[:, 0:2 * HC].rearrange("p (a c) -> p a c", c=HC)
        sqy = x_place[:, 2 * HC:4 * HC].rearrange("p (a c) -> p a c", c=HC)
        uu = x_place[:, 4 * HC:6 * HC].rearrange("p (a i d) -> p a i d", a=2, d=D)
        beta_o = x_place[:, 6 * HC:8 * HC].rearrange("p (a c) -> p a c", c=HC)
        ss = sb("ss", [P, 4, HT])
        sd = sb("sd", [P, 4, HT])
        coef = sb("coef", [P, 2, HT])
        coef2 = sb("coef2", [P, 2, HT])
        hid1 = gru[:, 0:4].rearrange("p (a b) c -> p a b c", b=2)
        sa = gru[:, 4:7]

        x_ld = [sem(f"x_ld{i}") for i in range(NT)]
        tok_ld = sem("tok_ld")
        gru_ld = sem("gru_ld")
        att_ld = sem("att_ld")
        m0_ld = sem("m0_ld")
        m1_ld = sem("m1_ld")
        consts = sem("consts")
        pool_step = sem("pool_step")
        dve_step = sem("dve_step")
        act_step = sem("act_step")
        tok_mm = sem("tok_mm")
        tok_ev = sem("tok_ev")
        ln_var = sem("ln_var")
        ln_rstd = sem("ln_rstd")
        xn_rdy = sem("xn_rdy")
        xt_mm = sem("xt_mm")
        xt_act = sem("xt_act")
        xl_rdy = sem("xl_rdy")
        gru_split = sem("gru_split")
        gru_mm = sem("gru_mm")
        gru_sig = sem("gru_sig")
        gru_scan = sem("gru_scan")
        gru_hb = sem("gru_hb")
        gru_out = sem("gru_out")
        gru_ev = sem("gru_ev")
        der_mm = sem("der_mm")
        der_hi = sem("der_hi")
        der_lo = sem("der_lo")
        bqk_rdy = sem("bqk_rdy")
        m0_prep = sem("m0_prep")
        gate_mm = sem("gate_mm")
        gate_ev = sem("gate_ev")
        gate_dif = sem("gate_dif")
        gate_sig = sem("gate_sig")
        comb_rdy = sem("comb_rdy")
        w1_rdy = sem("w1_rdy")
        h_mm = sem("h_mm")
        hid_rdy = sem("hid_rdy")
        y_mm = sem("y_mm")
        sq_rdy = sem("sq_rdy")
        ss_rdy = sem("ss_rdy")
        sd_rdy = sem("sd_rdy")
        cf_rdy = sem("cf_rdy")
        u_rdy = sem("u_rdy")
        added = sem("added")
        gT_mm = sem("gT_mm")
        gT_ev = sem("gT_ev")
        beta_mm = sem("beta_mm")
        beta_ev = sem("beta_ev")
        beta_add = sem("beta_add")
        q_mm = sem("q_mm")
        q_ev = sem("q_ev")
        r_mm = sem("r_mm")
        r_ev = sem("r_ev")
        s_mm = sem("s_mm")
        s_ev = sem("s_ev")
        s_sub = sem("s_sub")
        s_exp = sem("s_exp")
        px_rdy = sem("px_rdy")
        px_zero = sem("px_zero")
        v_mm = sem("v_mm")
        v_ev = sem("v_ev")
        av_mm = sem("av_mm")
        av_hb = sem("av_hb")
        av_ev = sem("av_ev")
        w13_rdy = sem("w13_rdy")
        a_mm = sem("a_mm")
        b_mm = sem("b_mm")
        silu_rdy = sem("silu_rdy")
        hid1_rdy = sem("hid1_rdy")
        y1_mm = sem("y1_mm")
        acc_rdy = sem("acc_rdy")
        out_st = sem("out_st")
        past = sem("past")

        blk = ctx.enter_context(nc.Block())

        def half(a, hf):
            return a[:, hf * HT:(hf + 1) * HT]

        def cols(hf):
            return slice(hf * HC, (hf + 1) * HC)

        def v3(ap, n):
            return ap.rearrange("p (a b) -> p a b", b=n)

        M0_LOADS, M1_LOADS, ATT_LOADS, GRU_LOADS = 7, 4, 5, 4
        DERIVED = 4
        M0_UNITS, M1_UNITS = 4, 6

        @blk.sync
        def _(sp):
            sp.dma_start(tok_w[:], t["tok_w"]).then_inc(tok_ld, 16)
            for i in range(NT):
                sp.dma_start(x_in[:, i], t["x"][i]).then_inc(x_ld[i], 16)
                if i == 1:
                    sp.dma_start(gru_w[:], t["gru_w"]).then_inc(gru_ld, 16)
            sp.dma_start(gru_wo[:], t["gru_wo"]).then_inc(gru_ld, 16)
            for dst, name in ((wqT, "wqT"), (wkT, "wkT"), (wvT, "wvT"), (wo, "wo")):
                sp.dma_start(dst, t[name]).then_inc(att_ld, 16)
            for dst, name in ((m0_w1, "m0_w1"), (m0_w2, "m0_w2")):
                sp.dma_start(dst[:], t[name]).then_inc(m0_ld, 16)
            sp.dma_start(m0_gamma[:], t["m0_gamma"].unsqueeze(0).broadcast_to([P, E0, D])).then_inc(m0_ld, 16)
            for dst, name in ((m1_w13, "m1_w13"), (m1_w2, "m1_w2")):
                sp.dma_start(dst[:], t[name]).then_inc(m1_ld, 16)
            for hf in range(HALVES):
                sp.wait_ge(acc_rdy, 2 + 2 * E1 - 1 + hf)
                sp.dma_start(out[hf * HC:(hf + 1) * HC, :].rearrange("(i p) d -> p i d", p=P),
                             half(h, hf)).then_inc(out_st, 16)
            sp.wait_ge(out_st, 16 * HALVES)

        @blk.gpsimd
        def _(g):
            steps = [0]

            def step(ins):
                steps[0] += 1
                ins.then_inc(pool_step, 1)
                g.wait_ge(pool_step, steps[0])

            g.sem_inc(added, 2)
            step(g.memset(ident[:], 0.0))
            step(g.affine_select(out=ident[:], in_=ident[:], compare_op=ALU.not_equal, fill=1.0, base=0,
                                 pattern=[[-1, P]], channel_multiplier=1))
            g.memset(expo[:], -0.5)
            g.memset(zero[:], 0.0)
            g.memset(eps_c[:], EPS)
            step(g.memset(ones[:], 1.0))
            step(g.tensor_copy(ones8r[:], ones[0:E0, :]))
            step(g.memset(block[:], 0.0))
            step(g.affine_select(out=block[:], in_=block[:], compare_op=ALU.is_ge, fill=MASKED, base=0,
                                 pattern=[[-SEQ, NT], [0, SEQ]], channel_multiplier=1))
            step(g.affine_select(out=block[:], in_=block[:], compare_op=ALU.is_ge, fill=MASKED, base=SEQ - 1,
                                 pattern=[[SEQ, NT], [0, SEQ]], channel_multiplier=-1))
            step(g.iota(iota_i[:], pattern=[[0, HT], [1, E0]], base=0, channel_multiplier=0))
            g.tensor_copy(iota8[:], iota_i[:]).then_inc(consts, 1)
            g.wait_ge(gru_ld, 16 * GRU_LOADS)
            step(g.tensor_tensor(gruH[:], gru_w[:], zero[:].broadcast_to([P, 4 * P]), ALU.add))
            g.tensor_tensor(gruL[:], gru_w[:], gruH[:].bitcast(F32), ALU.subtract).then_inc(gru_split, 1)

            def root(n, hf):
                g.wait_ge(ln_var, n + 1)
                g.tensor_tensor(half(rstd, hf), half(ve, hf), expo[:], ALU.pow).then_inc(ln_rstd, 1)

            def gru_bias(hf):
                g.wait_ge(tok_ev, HT * (hf + 1))
                g.tensor_tensor(half(hb, hf), half(h, hf), gru_bo[:].unsqueeze(1).broadcast_to([P, HT, D]),
                                ALU.add).then_inc(gru_hb, 1)

            root(0, 0)
            root(1, 1)
            gru_bias(0)
            gru_bias(1)
            g.wait_ge(tok_mm, NT)
            g.memset(PX[:], 0.0).then_inc(px_zero, 1)
            root(2, 0)
            g.wait_ge(m0_ld, 16 * M0_LOADS)

            def split_w1(e, slot):
                g.wait_ge(h_mm, 2 * e + 2)
                g.sem_inc(past, 1)
                g.tensor_tensor(w1H[:, slot], m0_w1[:, bass.ds(e, 1)].rearrange("p a n -> p (a n)"),
                                zero[:].broadcast_to([P, P]), ALU.add).then_inc(w1_rdy, 1)
                g.wait_ge(w1_rdy, 2 * e + 1)
                g.sem_inc(past, 1)
                g.tensor_tensor(w1L[:, slot], m0_w1[:, bass.ds(e, 1)].rearrange("p a n -> p (a n)"), w1H[:, slot].bitcast(F32), ALU.subtract).then_inc(w1_rdy, 1)

            split_w1(0, 0)
            root(3, 1)
            split_w1(1, 1)

            def add_unit(u, k):
                g.wait_ge(u_rdy, u + 5)
                g.wait_ge(added, u + 1)
                g.tensor_tensor(half(h, k % 2), half(h, k % 2), uu[:, k % 2], ALU.add).then_inc(added, 1)

            def m0_body(j, tail):
                for k in range(M0_UNITS):
                    if k % 2 == 0 and not tail:
                        split_w1(2 * j + 2 + k // 2, k // 2)
                    if tail and k == 2:
                        for hf in range(HALVES):
                            g.wait_ge(beta_ev, hf + 1)
                            g.wait_ge(added, 2 * E0 - 1 + hf)
                            g.tensor_tensor(half(h, hf), half(h, hf), v3(beta_o[:, hf], D), ALU.add).then_inc(beta_add, 1)
                        g.wait_ge(beta_add, HALVES)
                    add_unit(M0_UNITS * j + k, k)

            with g.Fori(0, E0 // 2 - 1) as j:
                m0_body(j, False)
            m0_body(E0 // 2 - 1, True)

            root(4, 0)
            root(5, 1)

            def split_w13(e, slot):
                g.wait_ge(b_mm, 4 * e + 4)
                g.sem_inc(past, 1)
                src = m1_w13[:, bass.ds(e, 1)].rearrange("p a c n -> p (a c n)")
                high = w13H[:, slot].rearrange("p c n -> p (c n)")
                low = w13L[:, slot].rearrange("p c n -> p (c n)")
                g.tensor_tensor(high, src, zero[:].broadcast_to([P, 4 * P]), ALU.add).then_inc(w13_rdy, 1)
                g.wait_ge(w13_rdy, 2 * e + 1)
                g.sem_inc(past, 1)
                g.tensor_tensor(low, src, high.bitcast(F32), ALU.subtract).then_inc(w13_rdy, 1)

            def att_bias(hf):
                g.wait_ge(added, 2 * E0 + 1 + hf)
                g.wait_ge(der_lo, DERIVED + 2)
                g.tensor_tensor(half(hb, hf), half(h, hf), att_ob[:].unsqueeze(1).broadcast_to([P, HT, D]),
                                ALU.add).then_inc(av_hb, 1)

            att_bias(0)
            att_bias(1)
            g.wait_ge(m1_ld, 16 * M1_LOADS)
            for e in range(3):
                split_w13(e, e)
            root(6, 0)
            root(7, 1)
            with g.Fori(1, E1 // 3) as j:
                for k in range(3):
                    split_w13(3 * j + k, k)

        @blk.scalar
        def _(act):
            act.sem_inc(hid_rdy, 2)
            act.sem_inc(sd_rdy, 4)
            for dst, name in ((gru_b, "gru_b"),):
                act.dma_start(dst[:], t[name]).then_inc(gru_ld, 16)
            act.dma_start(tok_b[:], t["tok_b"].unsqueeze(0).broadcast_to([P, D])).then_inc(tok_ld, 16)
            act.dma_start(gru_bo[:], t["gru_bo"].unsqueeze(0).broadcast_to([P, D])).then_inc(gru_ld, 16)
            act.dma_start(att_b[:], t["att_b"]).then_inc(att_ld, 16)
            for dst, name in ((m0_gate, "m0_gate"), (m0_b1, "m0_b1"), (m0_b2, "m0_b2"), (m0_beta, "m0_beta")):
                act.dma_start(dst[:], t[name]).then_inc(m0_ld, 16)
            act.dma_start(m1_gate[:], t["m1_gate"]).then_inc(m1_ld, 16)
            act.dma_start(m1_bias[:], t["m1_bias"].unsqueeze(0).broadcast_to([P, E0])).then_inc(m1_ld, 16)

            def evacuate_xt(n, hf):
                act.wait_ge(xt_mm, n + 1)
                act.activation(xH[:, cols(hf)], bank[7][:], ACT.Copy).then_inc(xt_act, 1)
                act.activation(xT[:, cols(hf)], bank[7][:], ACT.Copy).then_inc(xt_act, 1)

            def gru_sigmoids(hf):
                for c in range(HG):
                    act.wait_ge(gru_mm, HG * hf + c + 1)
                    if hf:
                        act.wait_ge(gru_scan, c + 1)
                    act.activation(gf[:, c], bank[2 + c][:], ACT.Sigmoid, bias=gru_bn[:, c:c + 1], scale=-1.0)
                    act.activation(gz[:, c], bank[2 + c][:], ACT.Sigmoid, bias=gru_b[:, 2 + c:3 + c])
                    act.activation(gs[:, c], bank[c][:], ACT.Sigmoid, bias=gru_b[:, c:c + 1]).then_inc(gru_sig, 1)

            def derived_high(i, dst):
                act.wait_ge(der_mm, i + 1)
                act.activation(dst, v3(bank[5 + i % 2][:], D), ACT.Copy).then_inc(der_hi, 1)

            evacuate_xt(0, 0)
            act.wait_ge(gru_ld, 16 * GRU_LOADS)
            act.wait_ge(dve_step, 1)
            gru_sigmoids(0)
            derived_high(0, GH[:, 0:4])
            derived_high(1, GH[:, 4:8])
            evacuate_xt(1, 1)
            gru_sigmoids(1)
            derived_high(2, UH[:, 0:4])
            derived_high(3, UH[:, 4:8])
            evacuate_xt(2, 0)

            def gate_sigmoid(hf):
                act.wait_ge(gate_dif, hf + 1)
                act.activation(gw2[:], gwt[:], ACT.Sigmoid).then_inc(gate_sig, 1)

            gate_sigmoid(0)
            evacuate_xt(3, 1)
            gate_sigmoid(1)

            def relu(u, e, k):
                act.wait_ge(h_mm, u + 5)
                act.wait_ge(y_mm, u + 1)
                act.sem_inc(past, 1)
                act.activation(hid0[:, k % 2], bank[4 + k % 2][:], ACT.Relu,
                               bias=m0_b1[:, bass.ds(e, 1)]).then_inc(hid_rdy, 1)

            def square(u, k):
                act.wait_ge(y_mm, u + 3)
                act.wait_ge(ss_rdy, u + 1)
                act.activation(sqy[:, k % 2], bank[k % 4][:], ACT.Square).then_inc(sq_rdy, 1)

            def deviation(u, k):
                act.wait_ge(ss_rdy, u + 3)
                act.wait_ge(u_rdy, u + 1)
                act.activation(sd[:, k % 4], ss[:, k % 4], ACT.Sqrt, scale=1.0 / D,
                               bias=eps_c[:, 0:1]).then_inc(sd_rdy, 1)

            act.wait_ge(m0_ld, 16 * M0_LOADS)
            relu(0, 0, 0)
            relu(1, 0, 1)
            square(0, 0)

            def m0_body(j, tail):
                for k in range(M0_UNITS):
                    u = M0_UNITS * j + k
                    if tail and k == 0:
                        for hf in range(HALVES):
                            act.wait_ge(beta_mm, hf + 1)
                            act.activation(beta_o[:, hf], bank[6][:], ACT.Copy).then_inc(beta_ev, 1)
                    if not tail or k + 2 < M0_UNITS:
                        relu(u + 2, 2 * j + (k + 2) // 2, k + 2)
                    if not tail or k + 1 < M0_UNITS:
                        square(u + 1, k + 1)
                    deviation(u, k)

            with act.Fori(0, E0 // 2 - 1) as j:
                m0_body(j, False)
            m0_body(E0 // 2 - 1, True)

            def q_out(hf):
                for i in range(NH):
                    act.wait_ge(q_mm, NH * hf + i + 1)
                    if i == 0 and hf:
                        act.wait_ge(s_mm, 2)
                    act.activation(qT[:, i], bank[i % 2][:], ACT.Identity,
                                   bias=att_small[:, i:i + 1]).then_inc(q_ev, 1)

            def exps(hf):
                for tp in range(2):
                    m = 2 * hf + tp
                    act.wait_ge(s_sub, m + 1)
                    act.activation(sq_[:, tp], sq_[:, tp], ACT.Exp).then_inc(s_exp, 1)

            def v_out(hf):
                for i in range(2 * HT):
                    act.wait_ge(v_mm, 2 * HT * hf + i + 1)
                    if hf:
                        act.wait_ge(av_mm, i // 2 + 1)
                    act.activation(V[:, i // 2, 4 * (i % 2):4 * (i % 2) + 4], v3(bank[4 + i % 2][:], D),
                                   ACT.Copy).then_inc(v_ev, 1)

            evacuate_xt(4, 0)
            q_out(0)
            exps(0)
            evacuate_xt(5, 1)
            q_out(1)
            v_out(0)
            exps(1)
            v_out(1)
            evacuate_xt(6, 0)

            def gate_exp(hf):
                act.wait_ge(gate_dif, HALVES + hf + 1)
                act.activation(gw2[:], gwt[:], ACT.Exp, scale=-1.0).then_inc(gate_sig, 1)

            gate_exp(0)
            evacuate_xt(7, 1)
            gate_exp(1)

            with act.Fori(0, E1 // 3) as j:
                for k in range(2 * M1_UNITS):
                    q = 2 * M1_UNITS * j + k
                    act.wait_ge(a_mm, q + 1)
                    act.wait_ge(hid1_rdy, q + 1)
                    act.activation(sa[:, k % 3], bank[k % 3][:], ACT.Silu).then_inc(silu_rdy, 1)

        @blk.tensor
        def _(pe):
            def three(dst, lh, ll, rh, rl, last=True):
                pe.matmul(dst, lh, rh, start=True, stop=False)
                pe.matmul(dst, lh, rl, start=False, stop=False)
                return pe.matmul(dst, ll, rh, start=False, stop=True)

            def transposes(n, hf):
                pe.wait_ge(xn_rdy, n + 1)
                if n:
                    pe.wait_ge(xt_act, 2 * n)
                    pe.wait_ge(xl_rdy, n)
                for i in range(HT):
                    ins = pe.transpose(bank[7][:, i * P:(i + 1) * P], xn[:, hf, i], ident[:])
                ins.then_inc(xt_mm, 1)

            def x_ready(n):
                pe.wait_ge(xt_act, 2 * (n + 1))
                pe.wait_ge(xl_rdy, n + 1)

            for s, n in ((h_mm, 4), (y_mm, 2), (b_mm, 12), (y1_mm, 2)):
                pe.sem_inc(s, n)
            pe.wait_ge(tok_ld, 32)
            pe.wait_ge(consts, 1)
            for i in range(NT):
                if i == NT - 1:
                    transposes(0, 0)
                pe.wait_ge(x_ld[i], 16)
                if i >= 2:
                    pe.wait_ge(tok_ev, i - 1)
                for c in range(KC):
                    ins = pe.matmul(bank[4 + i % 2][:, 0:D], x_in[:, i, c], tok_w[:, c],
                                    start=c == 0, stop=c == KC - 1)
                ins.then_inc(tok_mm, 1)

            def gru_in(hf):
                x_ready(hf)
                for c in range(HG):
                    if hf:
                        pe.wait_ge(gru_sig, c + 1)
                        pe.wait_ge(gru_scan, c + 1)
                    for b in (c, 2 + c):
                        ins = three(bank[b][:], gruH[:, b * P:(b + 1) * P], gruL[:, b * P:(b + 1) * P],
                                    xH[:, cols(hf)], xL[:, cols(hf)])
                    ins.then_inc(gru_mm, 1)

            def gru_project(hf):
                pe.wait_ge(gru_scan, HG * (hf + 1))
                if hf:
                    pe.wait_ge(gru_ev, 1)
                for i in range(HT):
                    for c in range(HG):
                        ins = pe.matmul(bank[4][:, i * D:(i + 1) * D], gh[:, c, i * P:(i + 1) * P], gru_wo[:, c],
                                        start=c == 0, stop=c == HG - 1)
                ins.then_inc(gru_out, 1)

            def derive(i, left, right):
                if i >= 2:
                    pe.wait_ge(der_hi, i - 1)
                    pe.wait_ge(der_lo, i - 1)
                for k in range(4):
                    n = 4 * (i % 2) + k
                    ins = pe.matmul(bank[5 + i % 2][:, k * D:(k + 1) * D], left[:, n], right[:, n],
                                    start=True, stop=True)
                ins.then_inc(der_mm, 1)

            pe.wait_ge(gru_split, 1)
            gru_in(0)
            pe.wait_ge(att_ld, 16 * ATT_LOADS)
            pe.wait_ge(tok_ev, NT)
            derive(0, wqT, wkT)
            derive(1, wqT, wkT)
            transposes(1, 1)
            gru_in(1)
            gru_project(0)
            derive(2, wvT, wo)
            derive(3, wvT, wo)
            gru_project(1)
            pe.wait_ge(der_hi, 3)
            pe.wait_ge(der_lo, 3)
            pe.wait_ge(bqk_rdy, 1)
            for n in range(NH):
                pe.matmul(bank[5][:, n:n + 1], wkT[:, n], att_b[:, 0, n:n + 1], start=True, stop=True)
                pe.matmul(bank[5][:, NH + n:NH + n + 1], wqT[:, n], att_b[:, 1, n:n + 1], start=True, stop=True)
            pe.matmul(bank[5][:, 2 * NH:3 * NH], ones[:], bqk[:], start=True, stop=True)
            for n in range(NH):
                ins = pe.matmul(bank[5][:, P:2 * P], att_b[:, 2, n:n + 1].broadcast_to([P, P]), wo[:, n],
                                start=n == 0, stop=n == NH - 1)
            ins.then_inc(der_mm, 1)

            def logits(stage, hf, weights):
                g = HALVES * stage + hf
                if g:
                    pe.wait_ge(gate_ev, g)
                for i in range(HT):
                    tok = (hf * HT + i) * P
                    ins = pe.matmul(bank[6][:, i * E0:(i + 1) * E0], xT[:, tok:tok + P], weights[:],
                                    start=True, stop=True)
                ins.then_inc(gate_mm, 1)

            transposes(2, 0)
            x_ready(2)
            pe.wait_ge(m0_ld, 16 * M0_LOADS)
            pe.wait_ge(der_hi, 4)
            pe.wait_ge(der_lo, 4)
            logits(0, 0, m0_gate)

            def w1_product(u, e, k):
                if k % 2 == 0:
                    pe.wait_ge(w1_rdy, 2 * e + 2)
                pe.wait_ge(hid_rdy, u + 1)
                s = (k // 2) % 2
                ins = three(bank[4 + k % 2][:], w1H[:, s], w1L[:, s], xH[:, cols(k % 2)], xL[:, cols(k % 2)])
                ins.then_inc(h_mm, 1)

            def w2_product(u, e, k):
                pe.wait_ge(hid_rdy, u + 3)
                pe.wait_ge(u_rdy, u + 1)
                pe.sem_inc(past, 1)
                y = v3(bank[k % 4][:], D)
                for part in (b2xH, b2xL):
                    pe.matmul(y, ones8r[:], part[:, bass.ds(e, 1)].broadcast_to([E0, HT, D]),
                              start=part is b2xH, stop=False, skip_group_check=True)
                for i in range(HT):
                    ins = pe.matmul(bank[k % 4][:, i * D:(i + 1) * D], hid0[:, k % 2, i * P:(i + 1) * P],
                                    w2c[:, bass.ds(e, 1)].rearrange("p a d -> p (a d)"),
                                    start=False, stop=i == HT - 1, skip_group_check=True)
                ins.then_inc(y_mm, 1)

            pe.wait_ge(gru_ev, HALVES)
            pe.wait_ge(der_lo, DERIVED + 2)
            pe.wait_ge(m0_prep, 1)
            w1_product(0, 0, 0)
            transposes(3, 1)
            x_ready(3)
            logits(0, 1, m0_gate)

            def m0_body(j, tail):
                for k in range(M0_UNITS):
                    u = M0_UNITS * j + k
                    if tail and k == 1:
                        pe.wait_ge(comb_rdy, HALVES)
                        pe.wait_ge(gate_ev, HALVES)
                        for hf in range(HALVES):
                            if hf:
                                pe.wait_ge(beta_ev, 1)
                            for i in range(HT):
                                ins = pe.matmul(bank[6][0:E0, i * P:(i + 1) * P], combt[:, hf * HT + i], ident[:],
                                                start=True, stop=True)
                            ins.then_inc(gT_mm, 1)
                            pe.wait_ge(gT_ev, hf + 1)
                            for i in range(HT):
                                ins = pe.matmul(bank[6][:, i * D:(i + 1) * D], gT[:, i * P:(i + 1) * P], m0_beta[:],
                                                start=True, stop=True)
                            ins.then_inc(beta_mm, 1)
                    if not tail or k + 1 < M0_UNITS:
                        w1_product(u + 1, 2 * j + (k + 1) // 2, k + 1)
                    w2_product(u, 2 * j + k // 2, k)

            with pe.Fori(0, E0 // 2 - 1) as j:
                m0_body(j, False)
            m0_body(E0 // 2 - 1, True)

            def q_project(n, hf):
                x_ready(n)
                for i in range(NH):
                    if NH * hf + i >= 2:
                        pe.wait_ge(q_ev, NH * hf + i - 1)
                    three(bank[i % 2][:], GH[:, i], GL[:, i], xH[:, cols(hf)], xL[:, cols(hf)]).then_inc(q_mm, 1)

            def r_project(hf):
                if hf:
                    pe.wait_ge(r_ev, hf)
                for i in range(HT):
                    tok = (hf * HT + i) * P
                    ins = pe.matmul(bank[6][:, i * NH:(i + 1) * NH], xT[:, tok:tok + P], att_small[:, NH:2 * NH],
                                    start=True, stop=True)
                ins.then_inc(r_mm, 1)

            def scores(hf):
                pe.wait_ge(q_ev, NH * (hf + 1))
                for tp in range(2):
                    if hf:
                        pe.wait_ge(s_ev, tp + 1)
                    for i in range(2):
                        for j in range(4):
                            c = (2 * tp + i) * P + BLK * j
                            tok = hf * HC + c
                            ins = pe.matmul(v3(bank[2 + tp][BLK * j:BLK * (j + 1), i * 256:(i + 1) * 256], BLK),
                                            xT[:, tok:tok + BLK], qT[:, :, c:c + BLK], start=True, stop=True,
                                            skip_group_check=True)
                    ins.then_inc(s_mm, 1)

            def values(hf):
                for i in range(HT):
                    tok = (hf * HT + i) * P
                    for c in range(2):
                        n = 2 * HT * hf + 2 * i + c
                        if n >= 2:
                            pe.wait_ge(v_ev, n - 1)
                        three(v3(bank[4 + c][:], D), xH[:, tok:tok + P], xL[:, tok:tok + P],
                              UH[:, 4 * c:4 * c + 4], UL[:, 4 * c:4 * c + 4]).then_inc(v_mm, 1)

            def attend(hf):
                pe.wait_ge(v_ev, 2 * HT * (hf + 1))
                pe.wait_ge(r_ev, HALVES)
                if hf:
                    pe.wait_ge(av_ev, 1)
                for i in range(HT):
                    pe.wait_ge(px_rdy, 4 * (HT * hf + i + 1))
                    for n in range(NH):
                        ins = pe.matmul(bank[6][:, i * D:(i + 1) * D], PX[:, i % 2, n], V[:, i, n],
                                        start=n == 0, stop=n == NH - 1)
                    ins.then_inc(av_mm, 1)

            transposes(4, 0)
            pe.wait_ge(u_rdy, 2 * E0 + 4)
            pe.wait_ge(hid_rdy, 2 * E0 + 2)
            pe.wait_ge(beta_ev, HALVES)
            q_project(4, 0)
            r_project(0)
            scores(0)
            transposes(5, 1)
            q_project(5, 1)
            r_project(1)
            scores(1)
            values(0)
            attend(0)
            values(1)
            transposes(6, 0)
            attend(1)

            def w13_products(u, e, k):
                if k % 2 == 0:
                    pe.wait_ge(w13_rdy, 2 * e + 2)
                s = (k // 2) % 3
                for c in range(2):
                    q, r = 2 * u + c, (2 * k + c) % 3
                    pe.wait_ge(hid1_rdy, q + 1)
                    three(bank[r][:], w13H[:, s, c], w13L[:, s, c], xH[:, cols(k % 2)],
                          xL[:, cols(k % 2)]).then_inc(a_mm, 1)
                    ins = three(bank[3 + r][:], w13H[:, s, 2 + c], w13L[:, s, 2 + c], xH[:, cols(k % 2)],
                                xL[:, cols(k % 2)])
                    ins.then_inc(b_mm, 1)

            def w2_products(u, e, k):
                pe.wait_ge(hid1_rdy, 2 * u + 5)
                pe.wait_ge(acc_rdy, u + 1)
                for i in range(HT):
                    for c in range(2):
                        ins = pe.matmul(bank[6 + k % 2][:, i * D:(i + 1) * D], hid1[:, k % 2, c, i * P:(i + 1) * P],
                                        m1_w2[:, bass.ds(e, 1), c].rearrange("p a d -> p (a d)"),
                                        start=c == 0, stop=c == 1)
                ins.then_inc(y1_mm, 1)

            x_ready(6)
            pe.wait_ge(m1_ld, 16 * M1_LOADS)
            pe.wait_ge(v_ev, 4 * HT)
            w13_products(0, 0, 0)
            pe.wait_ge(av_ev, HALVES)
            logits(1, 0, m1_gate)
            transposes(7, 1)
            x_ready(7)
            logits(1, 1, m1_gate)
            pe.wait_ge(gate_ev, 2 * HALVES)

            def m1_body(j, tail):
                for k in range(M1_UNITS):
                    u = M1_UNITS * j + k
                    if not tail or k + 1 < M1_UNITS:
                        w13_products(u + 1, 3 * j + (k + 1) // 2, k + 1)
                    w2_products(u, 3 * j + k // 2, k)

            with pe.Fori(0, E1 // 3 - 1) as j:
                m1_body(j, False)
            m1_body(E1 // 3 - 1, True)

        @blk.vector
        def _(v):
            steps = [0]

            def step(ins):
                steps[0] += 1
                ins.then_inc(dve_step, 1)
                v.wait_ge(dve_step, steps[0])

            def tile_stats(i):
                step(v.bn_stats(stats[:, i], h[:, i]))
                step(v.bn_aggr(mv[:, i], stats[:, i]))

            def variances(hf):
                v.tensor_scalar(half(ve, hf), half(mv, hf)[:, :, 1], EPS, None, ALU.add).then_inc(ln_var, 1)

            def half_stats(hf):
                for i in range(hf * HT, (hf + 1) * HT):
                    ins = v.bn_stats(stats[:, i], h[:, i])
                step(ins)
                for i in range(hf * HT, (hf + 1) * HT):
                    ins = v.bn_aggr(mv[:, i], stats[:, i])
                step(ins)
                variances(hf)

            def normalise(n, hf):
                v.wait_ge(ln_rstd, n + 1)
                if n >= 2:
                    v.wait_ge(xt_mm, n - 1)
                for i in range(HT):
                    ti = hf * HT + i
                    ins = v.tensor_scalar(xn[:, hf, i], h[:, ti], mv[:, ti, 0:1], rstd[:, ti:ti + 1],
                                          ALU.subtract, ALU.mult)
                ins.then_inc(xn_rdy, 1)

            def low_part(n, hf):
                v.wait_ge(xt_act, 2 * n + 2)
                v.tensor_tensor(xL[:, cols(hf)], xT[:, cols(hf)], xH[:, cols(hf)].bitcast(F32),
                                ALU.subtract).then_inc(xl_rdy, 1)

            for s, n in ((ss_rdy, 2), (u_rdy, 4), (hid1_rdy, 3), (acc_rdy, 2)):
                v.sem_inc(s, n)
            v.wait_ge(gru_ld, 16 * GRU_LOADS)
            step(v.tensor_scalar(gru_bn[:], gru_b[:, 2:4], -1.0, None, ALU.mult))
            step(v.tensor_scalar(gru_bh[:], gru_b[:, 0:2], 0.5, None, ALU.add))

            v.wait_ge(tok_ld, 32)
            for i in range(NT):
                v.wait_ge(tok_mm, i + 1)
                v.tensor_tensor(h[:, i], bank[4 + i % 2][:, 0:D], tok_b[:], ALU.add).then_inc(tok_ev, 1)
                v.wait_ge(tok_ev, i + 1)
                tile_stats(i)
                if i == HT - 1:
                    variances(0)
                if i == HT:
                    normalise(0, 0)
                if i == NT - 1:
                    variances(1)
            low_part(0, 0)
            normalise(1, 1)

            def gru_chunk(hf, c):
                k = HG * hf + c
                v.wait_ge(gru_sig, k + 1)
                step(v.scalar_tensor_tensor(gs[:, c], bank[c][:], gru_bh[:, c:c + 1], gs[:, c], ALU.add, ALU.max))
                v.memset(gf[:, c].rearrange("p (b s) -> p b s", s=SEQ)[:, :, 0:1], 0.0)
                step(v.tensor_tensor(gz[:, c], gz[:, c], gs[:, c], ALU.mult))
                if hf:
                    v.wait_ge(gru_out, 1)
                v.tensor_tensor_scan(gh[:, c], gf[:, c], gz[:, c], 0.0, ALU.mult, ALU.add).then_inc(gru_scan, 1)

            def derived_low(i, high, low):
                v.wait_ge(der_hi, i + 1)
                v.tensor_tensor(low, v3(bank[5 + i % 2][:], D), high.bitcast(F32), ALU.subtract).then_inc(der_lo, 1)

            def gru_residual(hf):
                v.wait_ge(gru_out, hf + 1)
                v.wait_ge(gru_hb, hf + 1)
                v.tensor_tensor(half(h, hf), v3(bank[4][:], D), half(hb, hf), ALU.add).then_inc(gru_ev, 1)
                v.wait_ge(gru_ev, hf + 1)

            gru_chunk(0, 0)
            gru_chunk(0, 1)
            v.wait_ge(att_ld, 16 * ATT_LOADS)
            v.tensor_tensor(bqk[:], att_b[:, 0], att_b[:, 1], ALU.mult).then_inc(bqk_rdy, 1)
            derived_low(0, GH[:, 0:4], GL[:, 0:4])
            derived_low(1, GH[:, 4:8], GL[:, 4:8])
            low_part(1, 1)
            v.wait_ge(gru_sig, HG + 1)
            step(v.scalar_tensor_tensor(gs[:, 0], bank[0][:], gru_bh[:, 0:1], gs[:, 0], ALU.add, ALU.max))
            v.memset(gf[:, 0].rearrange("p (b s) -> p b s", s=SEQ)[:, :, 0:1], 0.0)
            step(v.tensor_tensor(gz[:, 0], gz[:, 0], gs[:, 0], ALU.mult))
            v.wait_ge(gru_out, 1)
            v.tensor_tensor_scan(gh[:, 0], gf[:, 0], gz[:, 0], 0.0, ALU.mult, ALU.add).then_inc(gru_scan, 1)
            gru_chunk(1, 1)
            gru_residual(0)
            half_stats(0)
            derived_low(2, UH[:, 0:4], UL[:, 0:4])
            normalise(2, 0)
            derived_low(3, UH[:, 4:8], UL[:, 4:8])
            gru_residual(1)
            half_stats(1)
            v.wait_ge(der_mm, DERIVED + 1)
            v.tensor_copy(att_small[:], bank[5][:, 0:3 * NH]).then_inc(der_lo, 1)
            v.tensor_copy(att_ob[:], bank[5][:, P:2 * P]).then_inc(der_lo, 1)
            low_part(2, 0)
            normalise(3, 1)
            v.wait_ge(m0_ld, 16 * M0_LOADS)
            v.wait_ge(consts, 1)
            step(v.tensor_reduce(w2_mean[:], m0_w2[:], AX.X, ALU.add))
            step(v.tensor_scalar(w2_mean[:], w2_mean[:], 1.0 / D, None, ALU.mult))
            for n in range(2):
                s = slice(4 * n, 4 * n + 4)
                step(v.tensor_tensor(w2c[:, s], m0_w2[:, s], w2_mean[:, s].unsqueeze(2).broadcast_to([P, 4, D]),
                                     ALU.subtract))
            step(v.tensor_reduce(b2_mean[:], m0_b2[:], AX.X, ALU.add))
            step(v.tensor_scalar(b2_mean[:], b2_mean[:], 1.0 / D, None, ALU.mult))
            step(v.tensor_scalar(b2c[:], m0_b2[:], b2_mean[:], None, ALU.subtract))
            step(v.tensor_tensor(b2x[:], b2c[:].unsqueeze(1).broadcast_to([E0, E0, D]),
                                 ident[0:E0, 0:E0].unsqueeze(2).broadcast_to([E0, E0, D]), ALU.mult))
            step(v.tensor_copy(b2xH[:], b2x[:]))
            v.tensor_tensor(b2xL[:], b2x[:], b2xH[:].bitcast(F32), ALU.subtract).then_inc(m0_prep, 1)

            def one_hots(write):
                step(v.tensor_copy(idf[:], idx[:, :, 0:2]))
                for k in range(2):
                    step(v.tensor_tensor(eq[:], iota8[:], idf[:, :, k:k + 1].broadcast_to([P, HT, E0]), ALU.is_equal))
                    write(k)

            def gate0(hf):
                v.wait_ge(gate_mm, hf + 1)
                v.tensor_copy(lg[:], v3(bank[6][:, 0:HT * E0], E0)).then_inc(gate_ev, 1)
                v.wait_ge(gate_ev, hf + 1)
                for i in range(HT):
                    ins = v.max(top[:, i], lg[:, i])
                step(ins)
                for i in range(HT):
                    ins = v.max_index(idx[:, i], top[:, i], lg[:, i])
                step(ins)
                v.tensor_tensor(gwt[:, :, 0:1], top[:, :, 0:1], top[:, :, 1:2], ALU.subtract)
                v.tensor_tensor(gwt[:, :, 1:2], top[:, :, 1:2], top[:, :, 0:1], ALU.subtract).then_inc(gate_dif, 1)
                v.wait_ge(gate_sig, hf + 1)
                out_t = half(combt, hf)

                def write(k):
                    w = gw2[:, :, k:k + 1].broadcast_to([P, HT, E0])
                    if k == 0:
                        step(v.tensor_tensor(out_t, eq[:], w, ALU.mult))
                    else:
                        step(v.tensor_tensor(eq[:], eq[:], w, ALU.mult))
                        step(v.tensor_tensor(out_t, out_t, eq[:], ALU.add))

                one_hots(write)
                v.tensor_copy(comb0[:, :, hf * HT:(hf + 1) * HT], out_t.rearrange("p i e -> p e i")).then_inc(comb_rdy, 1)

            gate0(0)
            low_part(3, 1)
            gate0(1)
            v.wait_ge(comb_rdy, HALVES)

            def sums(u, k):
                v.wait_ge(sq_rdy, u + 1)
                v.wait_ge(sd_rdy, u + 1)
                v.tensor_reduce(ss[:, k % 4], v3(sqy[:, k % 2], D), AX.X, ALU.add).then_inc(ss_rdy, 1)

            def weigh(u, e, k):
                hf = k % 2
                v.wait_ge(sd_rdy, u + 5)
                v.reciprocal(coef[:, k % 2], sd[:, k % 4]).then_inc(cf_rdy, 1)
                v.wait_ge(cf_rdy, 2 * u + 1)
                v.tensor_tensor(coef2[:, k % 2], coef[:, k % 2],
                                comb0[:, bass.ds(e, 1), hf * HT:(hf + 1) * HT].rearrange("p a i -> p (a i)"),
                                ALU.mult).then_inc(cf_rdy, 1)
                v.wait_ge(cf_rdy, 2 * u + 2)
                v.wait_ge(added, u + 1)
                for i in range(HT):
                    ins = v.scalar_tensor_tensor(uu[:, k % 2, i], bank[k % 4][:, i * D:(i + 1) * D],
                                                 coef2[:, k % 2, i:i + 1],
                                                 m0_gamma[:, bass.ds(e, 1)].rearrange("p a d -> p (a d)"),
                                                 ALU.mult, ALU.mult)
                ins.then_inc(u_rdy, 1)

            sums(0, 0)

            def m0_body(j, tail):
                for k in range(M0_UNITS):
                    u = M0_UNITS * j + k
                    if tail and k == 0:
                        for hf in range(HALVES):
                            v.wait_ge(gT_mm, hf + 1)
                            if hf:
                                v.wait_ge(beta_mm, 1)
                            v.tensor_copy(gT[:], bank[6][0:E0, :]).then_inc(gT_ev, 1)
                    if not tail or k + 1 < M0_UNITS:
                        sums(u + 1, k + 1)
                    weigh(u, 2 * j + k // 2, k)

            with v.Fori(0, E0 // 2 - 1) as j:
                m0_body(j, False)
            m0_body(E0 // 2 - 1, True)

            for j in range(4):
                q = slice(BLK * j, BLK * (j + 1))
                ins = v.tensor_copy(mask[q, :, :].rearrange("p n (b s) -> p n b s", s=SEQ),
                                    block[q, 2 * j:2 * j + 2].unsqueeze(1).broadcast_to([BLK, 2 * NH, 2, SEQ]))
            step(ins)

            def query_constants(hf):
                v.wait_ge(r_mm, hf + 1)
                v.tensor_tensor(rr[:], v3(bank[6][:, 0:HT * NH], NH),
                                att_small[:, 2 * NH:3 * NH].unsqueeze(1).broadcast_to([P, HT, NH]),
                                ALU.add).then_inc(r_ev, 1)
                v.wait_ge(r_ev, hf + 1)
                step(v.tensor_scalar(rr[:], rr[:], SCALE, None, ALU.mult))

            def less_maximum(hf, tp):
                m = 2 * hf + tp
                v.wait_ge(s_mm, m + 1)
                v.scalar_tensor_tensor(sT[:].rearrange("p n b -> p (n b)"), bank[2 + tp][:], SCALE,
                                       mask[:].rearrange("p n b -> p (n b)"), ALU.mult, ALU.add).then_inc(s_ev, 1)
                v.wait_ge(s_ev, m + 1)
                step(v.transpose(sq_[:, tp].rearrange("p n b -> p (n b)"), sT[:].rearrange("p n b -> p (n b)")))
                step(v.tensor_reduce(row[:, 0], sq_[:, tp], AX.X, ALU.max))
                r = rr[:, 2 * tp:2 * tp + 2].rearrange("p i n -> p (i n)")
                step(v.tensor_tensor(row[:, 0], row[:, 0], r, ALU.add))
                step(v.tensor_tensor(row[:, 1], row[:, 0], r, ALU.subtract))
                v.tensor_tensor(sq_[:, tp], sq_[:, tp], row[:, 1].unsqueeze(2).broadcast_to([P, 2 * NH, BLK]),
                                ALU.subtract).then_inc(s_sub, 1)

            def probabilities(hf, tp):
                m = 2 * hf + tp
                v.wait_ge(s_exp, m + 1)
                step(v.tensor_reduce(row[:, 2], sq_[:, tp], AX.X, ALU.add))
                step(v.reciprocal(row[:, 3], row[:, 2]))
                step(v.tensor_tensor(sq_[:, tp], sq_[:, tp], row[:, 3].unsqueeze(2).broadcast_to([P, 2 * NH, BLK]),
                                     ALU.mult))
                for i in range(2):
                    ti = HT * hf + 2 * tp + i
                    if ti >= 2:
                        v.wait_ge(av_mm, ti - 1)
                    for j in range(4):
                        q = slice(BLK * j, BLK * (j + 1))
                        v.transpose(PX[q, i, :, BLK * j:BLK * (j + 1)],
                                    sq_[q, tp, NH * i:NH * (i + 1)]).then_inc(px_rdy, 1)

            v.wait_ge(px_zero, 1)
            v.wait_ge(added, 2 * E0 + 1)
            half_stats(0)
            normalise(4, 0)
            v.wait_ge(added, 2 * E0 + 2)
            half_stats(1)
            low_part(4, 0)
            normalise(5, 1)
            query_constants(0)
            less_maximum(0, 0)
            less_maximum(0, 1)
            low_part(5, 1)
            probabilities(0, 0)
            query_constants(1)
            less_maximum(1, 0)

            def att_residual(hf):
                v.wait_ge(av_mm, HT * (hf + 1))
                v.wait_ge(av_hb, hf + 1)
                v.tensor_tensor(half(h, hf), v3(bank[6][:], D), half(hb, hf), ALU.add).then_inc(av_ev, 1)
                v.wait_ge(av_ev, hf + 1)

            probabilities(0, 1)
            less_maximum(1, 1)
            att_residual(0)
            half_stats(0)
            normalise(6, 0)
            probabilities(1, 0)
            low_part(6, 0)
            probabilities(1, 1)
            att_residual(1)
            half_stats(1)
            normalise(7, 1)

            def gate1(hf):
                n = HALVES + hf
                v.wait_ge(gate_mm, n + 1)
                v.tensor_copy(lg[:], v3(bank[6][:, 0:HT * E0], E0)).then_inc(gate_ev, 1)
                v.wait_ge(gate_ev, n + 1)
                step(v.tensor_tensor(lgb[:], lg[:], m1_bias[:].unsqueeze(1).broadcast_to([P, HT, E0]), ALU.add))
                for i in range(HT):
                    v.max(top[:, i], lg[:, i])
                    ins = v.max(topb[:, i], lgb[:, i])
                step(ins)
                for i in range(HT):
                    v.max_index(idx[:, i], topb[:, i], lgb[:, i])
                v.tensor_copy(gwt[:], top[:, :, 0:2]).then_inc(gate_dif, 1)
                v.wait_ge(gate_sig, n + 1)
                step(v.tensor_scalar(gw2[:], gw2[:], 1.0, None, ALU.add))
                step(v.reciprocal(gw2[:], gw2[:]))
                step(v.tensor_reduce(row[:, 0, 0:HT], gw2[:], AX.X, ALU.add))
                step(v.reciprocal(row[:, 1, 0:HT], row[:, 0, 0:HT]))
                step(v.tensor_tensor(gw2[:], gw2[:], row[:, 1, 0:HT].unsqueeze(2).broadcast_to([P, HT, 2]), ALU.mult))

                def write(k):
                    w = gw2[:, :, k:k + 1].broadcast_to([P, HT, E0])
                    if k == 0:
                        step(v.tensor_tensor(lg[:], eq[:], w, ALU.mult))
                    else:
                        step(v.tensor_tensor(eq[:], eq[:], w, ALU.mult))
                        step(v.tensor_tensor(comb1[:, 1:E1, hf * HT:(hf + 1) * HT], lg[:].rearrange("p i e -> p e i"),
                                             eq[:].rearrange("p i e -> p e i"), ALU.add))

                one_hots(write)

            def gated(u, k):
                for c in range(2):
                    q, r = 2 * u + c, (2 * k + c) % 3
                    v.wait_ge(silu_rdy, q + 1)
                    v.wait_ge(b_mm, q + 13)
                    if c == 0:
                        v.wait_ge(y1_mm, u + 1)
                    v.tensor_tensor(hid1[:, k % 2, c], sa[:, r], bank[3 + r][:], ALU.mult).then_inc(hid1_rdy, 1)

            def accumulate(u, e, k):
                hf = k % 2
                v.wait_ge(y1_mm, u + 3)
                v.wait_ge(acc_rdy, u + 1)
                for i in range(HT):
                    ti = hf * HT + i
                    ins = v.scalar_tensor_tensor(h[:, ti], bank[6 + k % 2][:, i * D:(i + 1) * D],
                                                 comb1[:, bass.ds(e, 1), ti:ti + 1].rearrange("p a i -> p (a i)"),
                                                 h[:, ti], ALU.mult, ALU.add)
                ins.then_inc(acc_rdy, 1)

            step(v.memset(comb1[:, 0], 1.0))
            gate1(0)
            low_part(7, 1)
            gate1(1)
            gated(0, 0)

            def m1_body(j, tail):
                for k in range(M1_UNITS):
                    u = M1_UNITS * j + k
                    if not tail or k + 1 < M1_UNITS:
                        gated(u + 1, k + 1)
                    accumulate(u, 3 * j + k // 2, k)

            with v.Fori(0, E1 // 3 - 1) as j:
                m1_body(j, False)
            m1_body(E1 // 3 - 1, True)


def kernel(**inputs):
    import numpy as np
    import concourse.bacc as bacc
    from concourse.bass_utils import run_bass_kernel_spmd

    a = {k: np.asarray(v) for k, v in inputs.items()}
    B = a["x"].shape[0]
    x = a["x"].reshape(B, 3, 4, 16, 4, 16).transpose(1, 3, 5, 0, 2, 4).reshape(KC, P, NT, P).transpose(2, 1, 0, 3)
    host = {
        "x": x,
        "tok_w": a["L0_tok_W"].T.reshape(KC, P, D).transpose(1, 0, 2),
        "tok_b": a["L0_tok_b"],
        "gru_w": a["L0_attn_W_in"].T,
        "gru_b": a["L0_attn_b_in"].reshape(4, P).T,
        "gru_wo": a["L0_attn_W_out"].T.reshape(HG, P, D).transpose(1, 0, 2),
        "gru_bo": a["L0_attn_b_out"],
        "wqT": a["L1_attn_Wq"].transpose(2, 0, 1),
        "wkT": a["L1_attn_Wk"].transpose(2, 0, 1),
        "wvT": a["L1_attn_Wv"].transpose(2, 0, 1),
        "wo": a["L1_attn_Wo"].reshape(NH, P, D).transpose(1, 0, 2),
        "att_b": np.stack([a["L1_attn_bq"], a["L1_attn_bk"], a["L1_attn_bv"]]).transpose(2, 0, 1),
        "m0_gate": a["L0_ffn_Wg"],
        "m0_w1": a["L0_ffn_W1"].transpose(1, 0, 2),
        "m0_b1": a["L0_ffn_b1"].T,
        "m0_w2": a["L0_ffn_W2"].transpose(1, 0, 2),
        "m0_b2": a["L0_ffn_b2"],
        "m0_gamma": a["L0_ffn_gamma"],
        "m0_beta": a["L0_ffn_beta"],
        "m1_gate": a["L1_ffn_gate_w"].T,
        "m1_bias": a["L1_ffn_biases"],
        "m1_w13": np.concatenate([np.concatenate([a["L1_ffn_sw1"][None], a["L1_ffn_w1"]]),
                                  np.concatenate([a["L1_ffn_sw3"][None], a["L1_ffn_w3"]])],
                                 axis=2).transpose(1, 0, 2).reshape(D, E1, 4, P),
        "m1_w2": np.concatenate([a["L1_ffn_sw2"][None], a["L1_ffn_w2"]]).reshape(E1, 2, P, D).transpose(2, 0, 1, 3),
    }
    nc = bacc.Bacc("TRN2", target_bir_lowering=False, num_devices=1)
    arrays, aps = {}, {}
    for name, value in host.items():
        arrays[f"in_{name}"] = np.ascontiguousarray(value)
        aps[name] = nc.dram_tensor(f"in_{name}", arrays[f"in_{name}"].shape, mybir.dt.float32, kind="ExternalInput").ap()
    out = nc.dram_tensor("out", (TOK, D), mybir.dt.float32, kind="ExternalOutput").ap()
    build(nc, aps, out)
    r = run_bass_kernel_spmd(nc, [arrays], core_ids=[0])
    return r.results[0]["out"].reshape(B, SEQ, D)
```

```python
import concourse.bass as bass
from concourse import mybir
from contextlib import ExitStack

ALU = mybir.AluOpType
ACT = mybir.ActivationFunctionType
AX = mybir.AxisListType
F32 = mybir.dt.float32
F32R = mybir.dt.float32r
U32 = mybir.dt.uint32
I32 = mybir.dt.int32

P = 128
D = 128
TOK = 1024
NT = TOK // P
HALVES = 2
HT = NT // HALVES
HC = HT * P
SEQ = 16
KC = 6
HG = 2
E0 = 8
E1 = 9
NH = 8
EPS = 1e-5
SCALE = float(D) ** -0.5
MASKED = -1e30
BLK = 32
LOW = 32
B2_ROWS = 2 * LOW


def build(nc, t, out):
    with ExitStack() as ctx:
        def sb(name, shape, dt=F32):
            return ctx.enter_context(nc.sbuf_tensor(name, shape, dt))

        def sem(name):
            return ctx.enter_context(nc.semaphore(name))

        bank = [ctx.enter_context(nc.psum_tensor(f"bank{i}", [P, 512], F32)) for i in range(8)]

        x_in = sb("x_in", [P, NT, KC, P])
        x_place = x_in[:, :, :, :].rearrange("p i c k -> p (i c k)")
        tok_w = sb("tok_w", [P, KC, D])
        tok_b = sb("tok_b", [P, D])
        gru_w = sb("gru_w", [P, 4 * P])
        gru_b = sb("gru_b", [P, 4])
        gru_wo = sb("gru_wo", [P, HG, D])
        gru_bo = sb("gru_bo", [P, D])
        att_w = sb("att_w", [P, 4, NH, D])
        wqT, wkT, wvT, wo = (att_w[:, i] for i in range(4))
        att_b = sb("att_b", [P, 3, NH])
        m0_gate = sb("m0_gate", [P, E0])
        m0_w1 = sb("m0_w1", [P, E0, P])
        m0_b1 = sb("m0_b1", [P, E0])
        m0_w2 = sb("m0_w2", [P, E0, D])
        m0_b2 = sb("m0_b2", [B2_ROWS, D])
        m0_gamma = sb("m0_gamma", [P, E0, D])
        m0_beta = sb("m0_beta", [E0, D])
        m1_gate = sb("m1_gate", [P, E0])
        m1_bias = sb("m1_bias", [P, E0])
        m1_w13 = sb("m1_w13", [P, E1, 4, P])
        m1_w2 = sb("m1_w2", [P, E1, 2, D])

        ident = sb("ident", [P, P])
        ones = sb("ones", [P, P])
        ones_r = sb("ones_r", [B2_ROWS, P], F32R)
        pick = sb("pick", [B2_ROWS, E0])
        expo = sb("expo", [P, HT])
        own_img = sb("own_img", [P, BLK])
        other_img = sb("other_img", [P, BLK])
        iota_i = sb("iota_i", [P, NT, E0], I32)
        iota8 = sb("iota8", [P, NT, E0])
        eps_c = sb("eps_c", [P, 1])
        zero = sb("zero", [P, 1])

        gruH = sb("gruH", [P, 4 * P], F32R)
        gruL = sb("gruL", [P, 4 * P], F32R)
        gru_bn = sb("gru_bn", [P, HG])
        gru_bh = sb("gru_bh", [P, HG])
        GH = sb("GH", [P, NH, D], F32R)
        GL = sb("GL", [P, NH, D], F32R)
        UH = sb("UH", [P, NH, D], F32R)
        UL = sb("UL", [P, NH, D], F32R)
        bqk = sb("bqk", [P, NH])
        att_small = sb("att_small", [P, 3 * NH])
        att_ob = sb("att_ob", [P, D])
        w1H = sb("w1H", [P, 2, P], F32R)
        w1L = sb("w1L", [P, 2, P], F32R)
        w2_mean = sb("w2_mean", [P, E0])
        w2c = sb("w2c", [P, E0, D])
        b2_mean = sb("b2_mean", [B2_ROWS, 1])
        b2c = sb("b2c", [B2_ROWS, D])
        b2H = sb("b2H", [B2_ROWS, D], F32R)
        b2p = sb("b2p", [B2_ROWS, D])
        b2x = sb("b2x", [B2_ROWS, E0, D], F32R)
        w13H = sb("w13H", [P, 3, 4, P], F32R)
        w13L = sb("w13L", [P, 3, 4, P], F32R)

        h = sb("h", [P, NT, D])
        hb = sb("hb", [P, NT, D])
        stats = sb("stats", [P, NT, 6])
        mv = sb("mv", [P, NT, 2])
        ve = sb("ve", [P, NT])
        rstd = sb("rstd", [P, NT])
        xn = sb("xn", [P, HALVES, HT, D])
        xT = sb("xT", [P, TOK])
        xH = sb("xH", [P, TOK], F32R)
        xL = sb("xL", [P, TOK], F32R)
        gru = sb("gru", [P, 4 * HG, HC])
        gf = gru[:, 0:HG]
        gz = gru[:, HG:2 * HG]
        gs = gru[:, 2 * HG:3 * HG]
        gh = [gru[:, 3 * HG:4 * HG], x_place[:, 0:HG * HC].rearrange("p (a c) -> p a c", c=HC)]
        qT = att_w[:, :, :, :].rearrange("p a n d -> p (a n d)").rearrange("p (n c) -> p n c", c=HC)
        V = x_place[:, 0:HT * NH * D].rearrange("p (i n d) -> p i n d", n=NH, d=D)
        rr = sb("rr", [P, HT, NH])
        pT = sb("pT", [P, 2, 2 * NH, BLK])
        sq_ = sb("sq_", [P, 2, 2 * NH, BLK])
        row = sb("row", [P, 4, 2 * NH])
        px_place = [x_place[:, 8 * HC:12 * HC], gru[:, 0:4].rearrange("p a c -> p (a c)"),
                    gru[:, 4:8].rearrange("p a c -> p (a c)")]
        px_place = px_place + px_place[0:1]
        PX = [px_place[i // 2].rearrange("p (a n q) -> p a n q", a=2, q=P)[:, i % 2] for i in range(NT)]
        lg = sb("lg", [P, NT, E0])
        lgb = sb("lgb", [P, NT, E0])
        top = sb("top", [P, NT, 8])
        topb = sb("topb", [P, NT, 8])
        idx = sb("idx", [P, NT, 8], U32)
        idf = sb("idf", [P, NT, 2])
        gw2 = sb("gw2", [P, NT, 2])
        gwt = sb("gwt", [P, NT, 2])
        eq = sb("eq", [P, NT, E0])
        comb0 = sb("comb0", [P, E0, NT])
        comb1 = sb("comb1", [P, E1, NT])
        combt = sb("combt", [P, NT, E0])
        hid0 = x_place[:, 0:2 * HC].rearrange("p (a c) -> p a c", c=HC)
        gT = x_place[0:E0, 2 * HC:4 * HC].rearrange("p (a c) -> p a c", c=HC)
        uu = x_place[:, 4 * HC:6 * HC].rearrange("p (a i d) -> p a i d", a=2, d=D)
        beta_o = x_place[:, 6 * HC:8 * HC].rearrange("p (a c) -> p a c", c=HC)
        sqy = sb("sqy", [P, HT, D])
        ss = sb("ss", [P, 4, HT])
        sd = sb("sd", [P, 4, HT])
        coef = sb("coef", [P, 2, HT])
        inv = sb("inv", [P, 2, HT])
        hid1 = gru[:, 0:4].rearrange("p (a b) c -> p a b c", b=2)
        sa = gru[:, 4:7]

        x_ld = [sem(f"x_ld{i}") for i in range(NT)]
        tok_ld = sem("tok_ld")
        gru_w_ld = sem("gru_w_ld")
        gru_b_ld = sem("gru_b_ld")
        gru_o_ld = sem("gru_o_ld")
        att_qk_ld = sem("att_qk_ld")
        att_vo_ld = sem("att_vo_ld")
        m0_b2_ld = sem("m0_b2_ld")
        b2_zero = sem("b2_zero")
        m0_ld = sem("m0_ld")
        m1_ld = sem("m1_ld")
        consts = sem("consts")
        pool_step = sem("pool_step")
        dve_step = sem("dve_step")
        act_step = sem("act_step")
        tok_mm = sem("tok_mm")
        tok_ev = sem("tok_ev")
        ln_var = sem("ln_var")
        ln_rstd = sem("ln_rstd")
        xn_rdy = sem("xn_rdy")
        xt_mm = sem("xt_mm")
        xh_rdy = sem("xh_rdy")
        xl_rdy = sem("xl_rdy")
        xt_rdy = sem("xt_rdy")
        gru_split = sem("gru_split")
        gru_mm = sem("gru_mm")
        gru_sig = sem("gru_sig")
        gru_cand = sem("gru_cand")
        gru_scan = sem("gru_scan")
        gru_hb = sem("gru_hb")
        gru_out = sem("gru_out")
        gru_ev = sem("gru_ev")
        der_mm = sem("der_mm")
        der_hi = sem("der_hi")
        der_lo = sem("der_lo")
        small_mm = sem("small_mm")
        small_ev = sem("small_ev")
        bqk_rdy = sem("bqk_rdy")
        b2_parts = sem("b2_parts")
        b2x_rdy = sem("b2x_rdy")
        w2c_rdy = sem("w2c_rdy")
        gate_mm = sem("gate_mm")
        gate_ev = sem("gate_ev")
        gate_dif = sem("gate_dif")
        gate_sig = sem("gate_sig")
        comb_rdy = sem("comb_rdy")
        w1_high = sem("w1_high")
        w1_rdy = sem("w1_rdy")
        h_mm = sem("h_mm")
        hid_rdy = sem("hid_rdy")
        y_mm = sem("y_mm")
        ss_rdy = sem("ss_rdy")
        sd_rdy = sem("sd_rdy")
        inv_rdy = sem("inv_rdy")
        cf_rdy = sem("cf_rdy")
        u_rdy = sem("u_rdy")
        added = sem("added")
        last_added = sem("last_added")
        gT_mm = sem("gT_mm")
        gT_ev = sem("gT_ev")
        beta_mm = sem("beta_mm")
        beta_ev = sem("beta_ev")
        beta_add = sem("beta_add")
        q_mm = sem("q_mm")
        q_ev = sem("q_ev")
        r_mm = sem("r_mm")
        r_ev = sem("r_ev")
        s_mm = sem("s_mm")
        s_ev = sem("s_ev")
        s_sub = sem("s_sub")
        s_exp = sem("s_exp")
        pt_rdy = sem("pt_rdy")
        px_rdy = sem("px_rdy")
        px_zero = sem("px_zero")
        v_mm = sem("v_mm")
        v_ev = sem("v_ev")
        av_mm = sem("av_mm")
        av_hb = sem("av_hb")
        av_ev = sem("av_ev")
        w13_rdy = sem("w13_rdy")
        a_mm = sem("a_mm")
        b_mm = sem("b_mm")
        silu_rdy = sem("silu_rdy")
        hid1_rdy = sem("hid1_rdy")
        y1_mm = sem("y1_mm")
        acc_rdy = sem("acc_rdy")
        out_st = sem("out_st")
        past = sem("past")

        blk = ctx.enter_context(nc.Block())

        def half(a, hf):
            return a[:, hf * HT:(hf + 1) * HT]

        def cols(hf):
            return slice(hf * HC, (hf + 1) * HC)

        def v3(ap, n):
            return ap.rearrange("p (a b) -> p a b", b=n)

        M0_LOADS, M1_LOADS = 6, 4
        DERIVED = 4
        M0_UNITS, M1_UNITS = 4, 6

        @blk.sync
        def _(sp):
            sp.dma_start(tok_w[:], t["tok_w"]).then_inc(tok_ld, 16)
            for i in range(NT):
                sp.dma_start(x_in[:, i], t["x"][i]).then_inc(x_ld[i], 16)
                if i == 1:
                    sp.dma_start(gru_w[:], t["gru_w"]).then_inc(gru_w_ld, 16)
            for dst, name in ((wqT, "wqT"), (wkT, "wkT")):
                sp.dma_start(dst, t[name]).then_inc(att_qk_ld, 16)
            sp.dma_start(gru_wo[:], t["gru_wo"]).then_inc(gru_o_ld, 16)
            for dst, name in ((wvT, "wvT"), (wo, "wo")):
                sp.dma_start(dst, t[name]).then_inc(att_vo_ld, 16)
            for dst, name in ((m0_w1, "m0_w1"), (m0_w2, "m0_w2")):
                sp.dma_start(dst[:], t[name]).then_inc(m0_ld, 16)
            sp.dma_start(m0_gamma[:], t["m0_gamma"].unsqueeze(0).broadcast_to([P, E0, D])).then_inc(m0_ld, 16)
            for dst, name in ((m1_w13, "m1_w13"), (m1_w2, "m1_w2")):
                sp.dma_start(dst[:], t[name]).then_inc(m1_ld, 16)
            for hf in range(HALVES):
                sp.wait_ge(acc_rdy, 2 + 2 * E1 - 1 + hf)
                sp.dma_start(out[hf * HC:(hf + 1) * HC, :].rearrange("(i p) d -> p i d", p=P),
                             half(h, hf)).then_inc(out_st, 16)
            sp.wait_ge(out_st, 16 * HALVES)

        @blk.gpsimd
        def _(g):
            steps = [0]

            def step(ins):
                steps[0] += 1
                ins.then_inc(pool_step, 1)
                g.wait_ge(pool_step, steps[0])

            g.sem_inc(added, 2)
            g.memset(m0_b2[:], 0.0).then_inc(b2_zero, 1)
            step(g.memset(ident[:], 0.0))
            step(g.affine_select(out=ident[:], in_=ident[:], compare_op=ALU.not_equal, fill=1.0, base=0,
                                 pattern=[[-1, P]], channel_multiplier=1))
            g.memset(expo[:], -0.5)
            g.memset(zero[:], 0.0)
            g.memset(eps_c[:], EPS)
            step(g.memset(ones[:], 1.0))
            step(g.tensor_copy(ones_r[:], ones[0:B2_ROWS, :]))
            g.memset(own_img[:], 0.0)
            step(g.memset(other_img[:], 0.0))
            for row, cols_own, cols_other in ((0, slice(0, SEQ), slice(SEQ, BLK)), (LOW, slice(SEQ, BLK), slice(0, SEQ))):
                step(g.memset(own_img[row:row + 1, cols_own], 1.0))
                step(g.memset(other_img[row:row + 1, cols_other], MASKED))
            step(g.iota(iota_i[:], pattern=[[0, NT], [1, E0]], base=0, channel_multiplier=0))
            g.tensor_copy(iota8[:], iota_i[:]).then_inc(consts, 1)
            g.wait_ge(gru_w_ld, 16)
            step(g.tensor_tensor(gruH[:], gru_w[:], zero[:].broadcast_to([P, 4 * P]), ALU.add))
            g.tensor_tensor(gruL[:], gru_w[:], gruH[:].bitcast(F32), ALU.subtract).then_inc(gru_split, 1)

            def root(n, hf):
                g.wait_ge(ln_var, n + 1)
                g.tensor_tensor(half(rstd, hf), half(ve, hf), expo[:], ALU.pow).then_inc(ln_rstd, 1)

            def gru_bias(hf):
                g.wait_ge(gru_o_ld, 32)
                g.wait_ge(tok_ev, HT * (hf + 1))
                g.tensor_tensor(half(hb, hf), half(h, hf), gru_bo[:].unsqueeze(1).broadcast_to([P, HT, D]),
                                ALU.add).then_inc(gru_hb, 1)

            root(0, 0)
            root(1, 1)
            gru_bias(0)
            gru_bias(1)
            g.wait_ge(tok_mm, NT)
            g.memset(px_place[0], 0.0)
            root(2, 0)
            g.wait_ge(b2_parts, 1)
            g.tensor_tensor(b2x[:], b2p[:].unsqueeze(1).broadcast_to([B2_ROWS, E0, D]),
                            pick[:].unsqueeze(2).broadcast_to([B2_ROWS, E0, D]), ALU.mult).then_inc(b2x_rdy, 1)

            def split_w1(e, slot):
                g.wait_ge(h_mm, 2 * e + 2)
                g.sem_inc(past, 1)
                g.tensor_tensor(w1H[:, slot], m0_w1[:, bass.ds(e, 1)].rearrange("p a n -> p (a n)"),
                                zero[:].broadcast_to([P, P]), ALU.add).then_inc(w1_high, 1)
                g.wait_ge(w1_high, e + 1)
                g.sem_inc(past, 1)
                g.tensor_tensor(w1L[:, slot], m0_w1[:, bass.ds(e, 1)].rearrange("p a n -> p (a n)"),
                                w1H[:, slot].bitcast(F32), ALU.subtract).then_inc(w1_rdy, 1)

            g.wait_ge(m0_ld, 16 * M0_LOADS)
            split_w1(0, 0)
            root(3, 1)
            split_w1(1, 1)
            g.wait_ge(gru_out, 4)
            step(g.memset(px_place[1], 0.0))
            g.memset(px_place[2], 0.0).then_inc(px_zero, 1)
            split_w1(2, 0)

            def add_unit(u, k):
                g.wait_ge(u_rdy, u + 5)
                g.wait_ge(added, u + 1)
                g.tensor_tensor(half(h, k % 2), half(h, k % 2), uu[:, k % 2], ALU.add).then_inc(added, 1)

            def m0_body(j, more, tail):
                for k in range(2 if tail else M0_UNITS):
                    if k == 1 and not tail:
                        split_w1(2 * j + 3, 1)
                    if k == 3 and more:
                        split_w1(2 * j + 4, 0)
                    add_unit(M0_UNITS * j + k, k)
                    if tail:
                        g.wait_ge(beta_ev, k + 1)
                        g.wait_ge(added, M0_UNITS * j + k + 3)
                        g.tensor_tensor(half(h, k), half(h, k), v3(beta_o[:, k], D), ALU.add).then_inc(beta_add, 1)

            with g.Fori(0, E0 // 2 - 2) as j:
                m0_body(j, True, False)
            m0_body(E0 // 2 - 2, False, False)
            m0_body(E0 // 2 - 1, False, True)

            root(4, 0)
            root(5, 1)

            def split_w13(e, slot):
                g.wait_ge(b_mm, 4 * e + 4)
                g.sem_inc(past, 1)
                src = m1_w13[:, bass.ds(e, 1)].rearrange("p a c n -> p (a c n)")
                high = w13H[:, slot].rearrange("p c n -> p (c n)")
                low = w13L[:, slot].rearrange("p c n -> p (c n)")
                g.tensor_tensor(high, src, zero[:].broadcast_to([P, 4 * P]), ALU.add).then_inc(w13_rdy, 1)
                g.wait_ge(w13_rdy, 2 * e + 1)
                g.sem_inc(past, 1)
                g.tensor_tensor(low, src, high.bitcast(F32), ALU.subtract).then_inc(w13_rdy, 1)

            def att_bias(hf):
                g.wait_ge(last_added, hf + 1)
                g.wait_ge(small_ev, 1)
                g.tensor_tensor(half(hb, hf), half(h, hf), att_ob[:].unsqueeze(1).broadcast_to([P, HT, D]),
                                ALU.add).then_inc(av_hb, 1)

            att_bias(0)
            att_bias(1)
            g.wait_ge(m1_ld, 16 * M1_LOADS)
            for e in range(3):
                split_w13(e, e)
            root(6, 0)
            root(7, 1)
            with g.Fori(1, E1 // 3) as j:
                for k in range(3):
                    split_w13(3 * j + k, k)

        @blk.scalar
        def _(act):
            act.sem_inc(hid_rdy, 2)
            act.sem_inc(sd_rdy, 4)
            act.dma_start(gru_b[:], t["gru_b"]).then_inc(gru_b_ld, 16)
            act.dma_start(tok_b[:], t["tok_b"].unsqueeze(0).broadcast_to([P, D])).then_inc(tok_ld, 16)
            act.dma_start(gru_bo[:], t["gru_bo"].unsqueeze(0).broadcast_to([P, D])).then_inc(gru_o_ld, 16)
            act.dma_start(att_b[:], t["att_b"]).then_inc(att_qk_ld, 16)
            act.wait_ge(b2_zero, 1)
            for row in (0, LOW):
                act.dma_start(m0_b2[row:row + E0, :], t["m0_b2"]).then_inc(m0_b2_ld, 16)
            for dst, name in ((m0_gate, "m0_gate"), (m0_b1, "m0_b1"), (m0_beta, "m0_beta")):
                act.dma_start(dst[:], t[name]).then_inc(m0_ld, 16)
            act.dma_start(m1_gate[:], t["m1_gate"]).then_inc(m1_ld, 16)
            act.dma_start(m1_bias[:], t["m1_bias"].unsqueeze(0).broadcast_to([P, E0])).then_inc(m1_ld, 16)

            def high_part(n, hf):
                act.wait_ge(xt_mm, n + 1)
                act.activation(xH[:, cols(hf)], bank[7][:], ACT.Copy).then_inc(xh_rdy, 1)

            def whole(n, hf):
                act.wait_ge(xl_rdy, n + 1)
                act.activation(xT[:, cols(hf)], bank[7][:], ACT.Copy).then_inc(xt_rdy, 1)

            def gru_sigmoids(hf, c):
                act.wait_ge(gru_mm, HG * hf + c + 1)
                if hf:
                    act.wait_ge(gru_scan, c + 1)
                act.activation(gf[:, c], bank[2 + c][:], ACT.Sigmoid, bias=gru_bn[:, c:c + 1], scale=-1.0)
                act.activation(gz[:, c], bank[2 + c][:], ACT.Sigmoid, bias=gru_b[:, 2 + c:3 + c])
                act.activation(gs[:, c], bank[c][:], ACT.Sigmoid, bias=gru_b[:, c:c + 1]).then_inc(gru_sig, 1)

            def derived_high(i, dst):
                act.wait_ge(der_mm, i + 1)
                act.activation(dst, v3(bank[5 + i % 2][:], D), ACT.Copy).then_inc(der_hi, 1)

            act.preload_act_table(ACT.Sigmoid)
            high_part(0, 0)
            act.wait_ge(gru_b_ld, 16)
            act.wait_ge(dve_step, 1)
            gru_sigmoids(0, 0)
            high_part(1, 1)
            gru_sigmoids(0, 1)
            derived_high(0, GH[:, 0:4])
            derived_high(1, GH[:, 4:8])
            gru_sigmoids(1, 0)
            gru_sigmoids(1, 1)
            derived_high(2, UH[:, 0:4])
            derived_high(3, UH[:, 4:8])
            act.wait_ge(m0_ld, 16 * M0_LOADS)
            for e in range(E0):
                ins = act.activation(w2c[:, e], m0_w2[:, e], ACT.Copy, scale=-1.0 / D, accum_out=w2_mean[:, e:e + 1])
            ins.then_inc(act_step, 1)
            act.wait_ge(act_step, 1)
            for e in range(E0):
                ins = act.activation(w2c[:, e], m0_w2[:, e], ACT.Identity, bias=w2_mean[:, e:e + 1])
            ins.then_inc(w2c_rdy, 1)
            high_part(2, 0)
            whole(2, 0)

            def relu(u, e, k):
                act.wait_ge(h_mm, u + 5)
                act.wait_ge(y_mm, u + 1)
                act.sem_inc(past, 1)
                act.activation(hid0[:, k % 2], bank[4 + k % 2][:], ACT.Relu,
                               bias=m0_b1[:, bass.ds(e, 1)]).then_inc(hid_rdy, 1)

            def square(u, k, j=0):
                act.wait_ge(y_mm, u + 3)
                if k or j is not None:
                    act.wait_ge(ss_rdy, u)
                for i in range(HT):
                    ins = act.activation(sqy[:, i], bank[k % 4][:, i * D:(i + 1) * D], ACT.Square,
                                         accum_out=ss[:, k % 4, i:i + 1])
                ins.then_inc(ss_rdy, 1)

            def deviation(u, k):
                act.wait_ge(ss_rdy, u + 1)
                act.wait_ge(u_rdy, u + 1)
                act.activation(sd[:, k % 4], ss[:, k % 4], ACT.Sqrt, scale=1.0 / D,
                               bias=eps_c[:, 0:1]).then_inc(sd_rdy, 1)

            act.wait_ge(m0_ld, 16 * M0_LOADS)
            relu(0, 0, 0)
            square(0, 0, None)
            high_part(3, 1)
            whole(3, 1)
            relu(1, 0, 1)
            act.wait_ge(gate_dif, 1)
            act.activation(gw2[:], gwt[:], ACT.Sigmoid).then_inc(gate_sig, 1)
            act.preload_act_table(ACT.Sqrt)

            def m0_body(j, tail):
                for k in range(M0_UNITS):
                    u = M0_UNITS * j + k
                    if not tail or k + 2 < M0_UNITS:
                        relu(u + 2, 2 * j + (k + 2) // 2, k + 2)
                    if tail and k == 1:
                        for hf in range(HALVES):
                            act.wait_ge(beta_mm, hf + 1)
                            act.activation(beta_o[:, hf], bank[6 + hf][:], ACT.Copy).then_inc(beta_ev, 1)
                    if not tail or k + 1 < M0_UNITS:
                        square(u + 1, k + 1)
                    deviation(u, k)

            with act.Fori(0, E0 // 2 - 1) as j:
                m0_body(j, False)
            m0_body(E0 // 2 - 1, True)

            def q_out(hf, i):
                act.wait_ge(q_mm, NH * hf + i + 1)
                if i == 0 and hf:
                    act.wait_ge(s_mm, 2)
                act.activation(qT[:, i], bank[i % 2][:], ACT.Identity,
                               bias=att_small[:, i:i + 1]).then_inc(q_ev, 1)

            def exps(hf, tp):
                act.wait_ge(s_sub, 2 * hf + tp + 1)
                act.activation(sq_[:, tp], sq_[:, tp], ACT.Exp, scale=SCALE).then_inc(s_exp, 1)

            def spread(hf, tp):
                act.wait_ge(pt_rdy, 2 * hf + tp + 1)
                if hf and tp:
                    act.wait_ge(av_mm, 2)
                two = px_place[2 * hf + tp].rearrange("p (n q) -> p n q", q=P)
                for j in range(4):
                    q = slice(BLK * j, BLK * (j + 1))
                    act.activation(two[q, :, q], pT[q, tp], ACT.Copy).then_inc(px_rdy, 1)

            def v_out(hf, i):
                act.wait_ge(v_mm, 2 * HT * hf + i + 1)
                if hf:
                    act.wait_ge(av_mm, i // 2 + 1)
                act.activation(V[:, i // 2, 4 * (i % 2):4 * (i % 2) + 4], v3(bank[4 + i % 2][:], D),
                               ACT.Copy).then_inc(v_ev, 1)

            act.preload_act_table(ACT.Exp)
            act.wait_ge(small_mm, 1)
            act.activation(att_small[:], bank[5][:, 0:3 * NH], ACT.Copy)
            act.activation(att_ob[:], bank[5][:, P:2 * P], ACT.Copy).then_inc(small_ev, 1)
            act.wait_ge(small_ev, 1)
            high_part(4, 0)
            whole(4, 0)
            for i in range(NH // 2):
                q_out(0, i)
            high_part(5, 1)
            whole(5, 1)
            for i in range(NH // 2, NH):
                q_out(0, i)
            for i in range(NH):
                if i in (NH // 2, NH - 1):
                    exps(0, i // (NH - 1))
                q_out(1, i)
            act.wait_ge(px_zero, 1)
            for i in range(2 * HT):
                if i in (2, 5):
                    spread(0, i // 5)
                if i in (4, 7):
                    exps(1, i // 7)
                v_out(0, i)
            spread(1, 0)
            spread(1, 1)
            for i in range(2 * HT):
                v_out(1, i)
            high_part(6, 0)
            whole(6, 0)

            def silu(q, k):
                act.wait_ge(a_mm, q + 1)
                act.wait_ge(hid1_rdy, q + 1)
                act.activation(sa[:, k % 3], bank[k % 3][:], ACT.Silu).then_inc(silu_rdy, 1)

            silu(0, 0)
            silu(1, 1)
            high_part(7, 1)
            whole(7, 1)
            silu(2, 2)
            silu(3, 3)
            act.wait_ge(gate_dif, 2)
            act.activation(gw2[:], gwt[:], ACT.Exp, scale=-1.0).then_inc(gate_sig, 1)
            act.preload_act_table(ACT.Silu)

            AHEAD = 4

            def m1_body(j, tail):
                for k in range(2 * M1_UNITS - (AHEAD if tail else 0)):
                    silu(2 * M1_UNITS * j + k + AHEAD, k + AHEAD)

            with act.Fori(0, E1 // 3 - 1) as j:
                m1_body(j, False)
            m1_body(E1 // 3 - 1, True)

        @blk.tensor
        def _(pe):
            def three(dst, lh, ll, rh, rl, last=True):
                pe.matmul(dst, lh, rh, start=True, stop=False)
                pe.matmul(dst, lh, rl, start=False, stop=False)
                return pe.matmul(dst, ll, rh, start=False, stop=True)

            def transposes(n, hf):
                pe.wait_ge(xn_rdy, n + 1)
                if n:
                    pe.wait_ge(xl_rdy, n)
                if n > 2:
                    pe.wait_ge(xt_rdy, n - 2)
                for i in range(HT):
                    ins = pe.transpose(bank[7][:, i * P:(i + 1) * P], xn[:, hf, i], ident[:])
                ins.then_inc(xt_mm, 1)

            def x_ready(n):
                pe.wait_ge(xl_rdy, n + 1)

            for s, n in ((h_mm, 4), (y_mm, 2), (b_mm, 12), (y1_mm, 2)):
                pe.sem_inc(s, n)
            pe.wait_ge(tok_ld, 32)
            pe.wait_ge(consts, 1)
            for i in range(NT):
                if i == NT - 1:
                    transposes(0, 0)
                pe.wait_ge(x_ld[i], 16)
                if i >= 2:
                    pe.wait_ge(tok_ev, i - 1)
                for c in range(KC):
                    ins = pe.matmul(bank[4 + i % 2][:, 0:D], x_in[:, i, c], tok_w[:, c],
                                    start=c == 0, stop=c == KC - 1)
                ins.then_inc(tok_mm, 1)

            def gru_in(hf):
                x_ready(hf)
                for c in range(HG):
                    if hf:
                        pe.wait_ge(gru_sig, c + 1)
                        pe.wait_ge(gru_cand, c + 1)
                    for b in (c, 2 + c):
                        ins = three(bank[b][:], gruH[:, b * P:(b + 1) * P], gruL[:, b * P:(b + 1) * P],
                                    xH[:, cols(hf)], xL[:, cols(hf)])
                    ins.then_inc(gru_mm, 1)

            def gru_project(hf):
                pe.wait_ge(gru_scan, HG * (hf + 1))
                pe.wait_ge(gru_o_ld, 32)
                for i in range(HT):
                    dst = bank[4][:] if hf == 0 else bank[i // 2][:]
                    for c in range(HG):
                        ins = pe.matmul(dst[:, i * D:(i + 1) * D], gh[hf][:, c, i * P:(i + 1) * P], gru_wo[:, c],
                                        start=c == 0, stop=c == HG - 1)
                    if i % 2:
                        ins.then_inc(gru_out, 1)

            def derive(i, left, right):
                if i >= 2:
                    pe.wait_ge(der_hi, i - 1)
                    pe.wait_ge(der_lo, i - 1)
                for k in range(4):
                    n = 4 * (i % 2) + k
                    ins = pe.matmul(bank[5 + i % 2][:, k * D:(k + 1) * D], left[:, n], right[:, n],
                                    start=True, stop=True)
                ins.then_inc(der_mm, 1)

            pe.wait_ge(gru_split, 1)
            gru_in(0)
            transposes(1, 1)
            pe.wait_ge(att_qk_ld, 16 * 3)
            pe.wait_ge(tok_ev, NT)
            derive(0, wqT, wkT)
            derive(1, wqT, wkT)
            gru_in(1)
            gru_project(0)
            pe.wait_ge(att_vo_ld, 16 * 2)
            derive(2, wvT, wo)
            derive(3, wvT, wo)
            gru_project(1)
            def logits(stage, hf, weights):
                pe.wait_ge(xt_rdy, HALVES * 2 * stage + hf + 1)
                for i in range(hf * HT, (hf + 1) * HT):
                    ins = pe.matmul(bank[6 + stage][:, i * E0:(i + 1) * E0], xT[:, i * P:(i + 1) * P], weights[:],
                                    start=True, stop=True)
                if hf:
                    ins.then_inc(gate_mm, 1)

            transposes(2, 0)
            pe.wait_ge(m0_ld, 16 * M0_LOADS)
            def w1_product(u, e, k):
                if k % 2 == 0:
                    pe.wait_ge(w1_rdy, e + 1)
                pe.wait_ge(hid_rdy, u + 1)
                s = (k // 2) % 2
                ins = three(bank[4 + k % 2][:], w1H[:, s], w1L[:, s], xH[:, cols(k % 2)], xL[:, cols(k % 2)])
                ins.then_inc(h_mm, 1)

            def w2_product(u, e, k):
                pe.wait_ge(hid_rdy, u + 3)
                pe.wait_ge(u_rdy, u + 1)
                pe.sem_inc(past, 1)
                y = v3(bank[k % 4][:], D)
                pe.matmul(y, ones_r[:], b2x[:, bass.ds(e, 1)].broadcast_to([B2_ROWS, HT, D]),
                          start=True, stop=False, skip_group_check=True)
                for i in range(HT):
                    ins = pe.matmul(bank[k % 4][:, i * D:(i + 1) * D], hid0[:, k % 2, i * P:(i + 1) * P],
                                    w2c[:, bass.ds(e, 1)].rearrange("p a d -> p (a d)"),
                                    start=False, stop=i == HT - 1, skip_group_check=True)
                ins.then_inc(y_mm, 1)

            pe.wait_ge(gru_ev, 2)
            x_ready(2)
            w1_product(0, 0, 0)
            pe.wait_ge(w2c_rdy, 1)
            pe.wait_ge(b2x_rdy, 1)
            pe.wait_ge(gru_ev, 4)
            w2_product(0, 0, 0)
            transposes(3, 1)
            pe.wait_ge(der_hi, 4)
            pe.wait_ge(der_lo, 4)
            logits(0, 0, m0_gate)
            x_ready(3)
            w1_product(1, 0, 1)
            logits(0, 1, m0_gate)

            def m0_body(j, tail):
                for k in range(M0_UNITS):
                    u = M0_UNITS * j + k
                    if tail and k == 0:
                        pe.wait_ge(comb_rdy, 1)
                        pe.wait_ge(xt_rdy, 2)
                        for i in range(NT):
                            ins = pe.matmul(bank[6 + i // HT][0:E0, i % HT * P:(i % HT + 1) * P], combt[:, i], ident[:],
                                            start=True, stop=True)
                            if i % HT == HT - 1:
                                ins.then_inc(gT_mm, 1)
                    if tail and k == 1:
                        for hf in range(HALVES):
                            pe.wait_ge(gT_ev, hf + 1)
                            for i in range(HT):
                                ins = pe.matmul(bank[6 + hf][:, i * D:(i + 1) * D], gT[:, hf, i * P:(i + 1) * P],
                                                m0_beta[:], start=True, stop=True)
                            ins.then_inc(beta_mm, 1)
                    if not tail or k + 2 < M0_UNITS:
                        w1_product(u + 2, 2 * j + (k + 2) // 2, k + 2)
                    if not tail or k + 1 < M0_UNITS:
                        w2_product(u + 1, 2 * j + (k + 1) // 2, k + 1)

            with pe.Fori(0, E0 // 2 - 1) as j:
                m0_body(j, False)
            m0_body(E0 // 2 - 1, True)

            def q_project(hf, heads):
                for i in heads:
                    if NH * hf + i >= 2:
                        pe.wait_ge(q_ev, NH * hf + i - 1)
                    three(bank[i % 2][:], GH[:, i], GL[:, i], xH[:, cols(hf)], xL[:, cols(hf)]).then_inc(q_mm, 1)

            def r_project(hf):
                pe.wait_ge(xt_rdy, HALVES + hf + 1)
                pe.wait_ge(small_ev, 1)
                if hf:
                    pe.wait_ge(r_ev, hf)
                for i in range(HT):
                    tok = (hf * HT + i) * P
                    ins = pe.matmul(bank[6][:, i * NH:(i + 1) * NH], xT[:, tok:tok + P], att_small[:, NH:2 * NH],
                                    start=True, stop=True)
                ins.then_inc(r_mm, 1)

            def scores(hf):
                pe.wait_ge(q_ev, NH * (hf + 1))
                for tp in range(2):
                    if hf:
                        pe.wait_ge(s_ev, tp + 1)
                    for i in range(2):
                        for j in range(4):
                            c = (2 * tp + i) * P + BLK * j
                            tok = hf * HC + c
                            ins = pe.matmul(v3(bank[2 + tp][BLK * j:BLK * (j + 1), i * 256:(i + 1) * 256], BLK),
                                            xT[:, tok:tok + BLK], qT[:, :, c:c + BLK], start=True, stop=False,
                                            skip_group_check=True)
                        for j in range(4):
                            ins = pe.matmul(v3(bank[2 + tp][BLK * j:BLK * (j + 1), i * 256:(i + 1) * 256], BLK),
                                            own_img[:], other_img[:].unsqueeze(1).broadcast_to([P, NH, BLK]),
                                            start=False, stop=True, skip_group_check=True)
                    ins.then_inc(s_mm, 1)

            def values(hf, tiles):
                for i in tiles:
                    tok = (hf * HT + i) * P
                    for c in range(2):
                        n = 2 * HT * hf + 2 * i + c
                        if n >= 2:
                            pe.wait_ge(v_ev, n - 1)
                        three(v3(bank[4 + c][:], D), xH[:, tok:tok + P], xL[:, tok:tok + P],
                              UH[:, 4 * c:4 * c + 4], UL[:, 4 * c:4 * c + 4]).then_inc(v_mm, 1)

            def attend(hf):
                pe.wait_ge(v_ev, 2 * HT * (hf + 1))
                pe.wait_ge(r_ev, HALVES)
                pe.wait_ge(s_ev, 2 + hf)
                for i in range(HT):
                    if i % 2 == 0:
                        pe.wait_ge(px_rdy, 4 * (2 * hf + i // 2 + 1))
                    if hf and i == 2:
                        pe.wait_ge(av_ev, 2)
                    dst = bank[2 if hf and i < 2 else 6][:]
                    for n in range(NH):
                        ins = pe.matmul(dst[:, i * D:(i + 1) * D], PX[hf * HT + i][:, n], V[:, i, n],
                                        start=n == 0, stop=n == NH - 1)
                    ins.then_inc(av_mm, 1)

            pe.wait_ge(bqk_rdy, 1)
            pe.wait_ge(hid_rdy, 2 * E0 + 2)
            for n in range(NH):
                pe.matmul(bank[5][:, n:n + 1], wkT[:, n], att_b[:, 0, n:n + 1], start=True, stop=True)
                pe.matmul(bank[5][:, NH + n:NH + n + 1], wqT[:, n], att_b[:, 1, n:n + 1], start=True, stop=True)
            pe.matmul(bank[5][:, 2 * NH:3 * NH], ones[:], bqk[:], start=True, stop=True)
            for n in range(NH):
                ins = pe.matmul(bank[5][:, P:2 * P], att_b[:, 2, n:n + 1].broadcast_to([P, P]), wo[:, n],
                                start=n == 0, stop=n == NH - 1)
            ins.then_inc(small_mm, 1)

            transposes(4, 0)
            pe.wait_ge(u_rdy, 2 * E0 + 4)
            pe.wait_ge(beta_ev, HALVES)
            x_ready(4)
            q_project(0, range(NH // 2))
            transposes(5, 1)
            q_project(0, range(NH // 2, NH))
            r_project(0)
            scores(0)
            x_ready(5)
            r_project(1)
            q_project(1, range(NH))
            values(0, [0])
            scores(1)
            values(0, range(1, HT))
            attend(0)
            values(1, range(HT))
            transposes(6, 0)
            attend(1)

            def w13_products(u, e, k):
                if k % 2 == 0:
                    pe.wait_ge(w13_rdy, 2 * e + 2)
                s = (k // 2) % 3
                for c in range(2):
                    q, r = 2 * u + c, (2 * k + c) % 3
                    pe.wait_ge(hid1_rdy, q + 1)
                    three(bank[r][:], w13H[:, s, c], w13L[:, s, c], xH[:, cols(k % 2)],
                          xL[:, cols(k % 2)]).then_inc(a_mm, 1)
                    ins = three(bank[3 + r][:], w13H[:, s, 2 + c], w13L[:, s, 2 + c], xH[:, cols(k % 2)],
                                xL[:, cols(k % 2)])
                    ins.then_inc(b_mm, 1)

            def w2_products(u, e, k):
                pe.wait_ge(hid1_rdy, 2 * u + 5)
                pe.wait_ge(acc_rdy, u + 1)
                for i in range(HT):
                    for c in range(2):
                        ins = pe.matmul(bank[6 + k % 2][:, i * D:(i + 1) * D], hid1[:, k % 2, c, i * P:(i + 1) * P],
                                        m1_w2[:, bass.ds(e, 1), c].rearrange("p a d -> p (a d)"),
                                        start=c == 0, stop=c == 1)
                ins.then_inc(y1_mm, 1)

            x_ready(6)
            pe.wait_ge(m1_ld, 16 * M1_LOADS)
            pe.wait_ge(v_ev, 4 * HT)
            w13_products(0, 0, 0)
            transposes(7, 1)
            pe.wait_ge(av_ev, 2 * HALVES)
            w2_products(0, 0, 0)
            x_ready(7)
            w13_products(1, 0, 1)
            pe.wait_ge(xt_rdy, 6)
            logits(1, 0, m1_gate)
            logits(1, 1, m1_gate)
            pe.wait_ge(gate_ev, 2)

            def m1_body(j, tail):
                for k in range(M1_UNITS):
                    u = M1_UNITS * j + k
                    if not tail or k + 2 < M1_UNITS:
                        w13_products(u + 2, 3 * j + (k + 2) // 2, k + 2)
                    if not tail or k + 1 < M1_UNITS:
                        w2_products(u + 1, 3 * j + (k + 1) // 2, k + 1)

            with pe.Fori(0, E1 // 3 - 1) as j:
                m1_body(j, False)
            m1_body(E1 // 3 - 1, True)

        @blk.vector
        def _(v):
            steps = [0]

            def step(ins):
                steps[0] += 1
                ins.then_inc(dve_step, 1)
                v.wait_ge(dve_step, steps[0])

            def tile_stats(i):
                step(v.bn_stats(stats[:, i], h[:, i]))
                step(v.bn_aggr(mv[:, i], stats[:, i]))

            def variances(hf):
                v.tensor_scalar(half(ve, hf), half(mv, hf)[:, :, 1], EPS, None, ALU.add).then_inc(ln_var, 1)

            def half_stats(hf):
                for i in range(hf * HT, (hf + 1) * HT):
                    ins = v.bn_stats(stats[:, i], h[:, i])
                step(ins)
                for i in range(hf * HT, (hf + 1) * HT):
                    ins = v.bn_aggr(mv[:, i], stats[:, i])
                step(ins)
                variances(hf)

            def normalise(n, hf):
                v.wait_ge(ln_rstd, n + 1)
                if n >= 2:
                    v.wait_ge(xt_mm, n - 1)
                for i in range(HT):
                    ti = hf * HT + i
                    ins = v.tensor_scalar(xn[:, hf, i], h[:, ti], mv[:, ti, 0:1], rstd[:, ti:ti + 1],
                                          ALU.subtract, ALU.mult)
                ins.then_inc(xn_rdy, 1)

            def low_part(n, hf):
                v.wait_ge(xh_rdy, n + 1)
                v.tensor_tensor(xL[:, cols(hf)], bank[7][:], xH[:, cols(hf)].bitcast(F32),
                                ALU.subtract).then_inc(xl_rdy, 1)

            def residual(hf, banks, made, per_two, biased, taken, meanwhile=None):
                for i in range(0, HT, 2):
                    n = (hf * HT + i) // 2
                    tiles = slice(hf * HT + i, hf * HT + i + 2)
                    v.wait_ge(made, per_two * (n + 2 if banks[0] is banks[1] and i == 0 else n + 1))
                    v.wait_ge(biased, hf + 1)
                    v.tensor_tensor(h[:, tiles], v3(banks[i // 2][:, i * D:(i + 2) * D], D), hb[:, tiles],
                                    ALU.add).then_inc(taken, 1)
                    v.wait_ge(taken, n + 1)
                    for k in range(hf * HT + i, hf * HT + i + 2):
                        ins = v.bn_stats(stats[:, k], h[:, k])
                    step(ins)
                    if meanwhile and i == 0:
                        meanwhile()
                for i in range(hf * HT, (hf + 1) * HT):
                    ins = v.bn_aggr(mv[:, i], stats[:, i])
                step(ins)
                variances(hf)

            for s, n in ((u_rdy, 4), (hid1_rdy, 3), (acc_rdy, 2)):
                v.sem_inc(s, n)
            v.wait_ge(gru_b_ld, 16)
            step(v.tensor_scalar(gru_bn[:], gru_b[:, 2:4], -1.0, None, ALU.mult))
            step(v.tensor_scalar(gru_bh[:], gru_b[:, 0:2], 0.5, None, ALU.add))
            v.wait_ge(consts, 1)
            for row0 in (0, LOW):
                ins = v.tensor_copy(pick[row0:row0 + BLK, :], ident[row0:row0 + BLK, row0:row0 + E0])
            step(ins)

            v.wait_ge(tok_ld, 32)
            for i in range(NT):
                if i == NT - 1:
                    low_part(0, 0)
                v.wait_ge(tok_mm, i + 1)
                v.tensor_tensor(h[:, i], bank[4 + i % 2][:, 0:D], tok_b[:], ALU.add).then_inc(tok_ev, 1)
                v.wait_ge(tok_ev, i + 1)
                tile_stats(i)
                if i == 1:
                    v.wait_ge(m0_b2_ld, 16 * 2)
                    step(v.tensor_reduce(b2_mean[:], m0_b2[:], AX.X, ALU.add))
                    step(v.tensor_scalar(b2_mean[:], b2_mean[:], 1.0 / D, None, ALU.mult))
                    step(v.tensor_scalar(b2c[:], m0_b2[:], b2_mean[:], None, ALU.subtract))
                    step(v.tensor_copy(b2H[:], b2c[:]))
                    v.tensor_copy(b2p[0:LOW, :], b2H[0:LOW, :].bitcast(F32))
                    v.tensor_tensor(b2p[LOW:2 * LOW, :], b2c[LOW:2 * LOW, :], b2H[LOW:2 * LOW, :].bitcast(F32),
                                    ALU.subtract).then_inc(b2_parts, 1)
                if i == HT - 1:
                    variances(0)
                if i == HT:
                    normalise(0, 0)
                if i == NT - 1:
                    variances(1)
            normalise(1, 1)

            def gru_chunk(hf, c, meanwhile=None):
                k = HG * hf + c
                v.wait_ge(gru_sig, k + 1)
                v.scalar_tensor_tensor(gs[:, c], bank[c][:], gru_bh[:, c:c + 1], gs[:, c],
                                       ALU.add, ALU.max).then_inc(gru_cand, 1)
                if meanwhile:
                    meanwhile()
                v.wait_ge(gru_cand, k + 1)
                v.memset(gf[:, c].rearrange("p (b s) -> p b s", s=SEQ)[:, :, 0:1], 0.0)
                step(v.tensor_tensor(gz[:, c], gz[:, c], gs[:, c], ALU.mult))
                v.tensor_tensor_scan(gh[hf][:, c], gf[:, c], gz[:, c], 0.0, ALU.mult, ALU.add).then_inc(gru_scan, 1)

            def derived_low(i, high, low):
                v.wait_ge(der_hi, i + 1)
                v.tensor_tensor(low, v3(bank[5 + i % 2][:], D), high.bitcast(F32), ALU.subtract).then_inc(der_lo, 1)

            gru_chunk(0, 0, lambda: low_part(1, 1))
            gru_chunk(0, 1)
            v.wait_ge(att_qk_ld, 16 * 3)
            v.tensor_tensor(bqk[:], att_b[:, 0], att_b[:, 1], ALU.mult).then_inc(bqk_rdy, 1)
            derived_low(0, GH[:, 0:4], GL[:, 0:4])
            derived_low(1, GH[:, 4:8], GL[:, 4:8])
            gru_chunk(1, 0)
            gru_chunk(1, 1)
            residual(0, [bank[4], bank[4]], gru_out, 1, gru_hb, gru_ev)
            derived_low(2, UH[:, 0:4], UL[:, 0:4])
            normalise(2, 0)
            derived_low(3, UH[:, 4:8], UL[:, 4:8])
            residual(1, [bank[0], bank[1]], gru_out, 1, gru_hb, gru_ev, lambda: low_part(2, 0))
            normalise(3, 1)
            def one_hots(write):
                step(v.tensor_copy(idf[:], idx[:, :, 0:2]))
                for k in range(2):
                    step(v.tensor_tensor(eq[:], iota8[:], idf[:, :, k:k + 1].broadcast_to([P, NT, E0]), ALU.is_equal))
                    write(k)

            low_part(3, 1)
            v.wait_ge(gate_mm, 1)
            v.tensor_copy(lg[:], v3(bank[6][:, 0:NT * E0], E0)).then_inc(gate_ev, 1)
            v.wait_ge(gate_ev, 1)
            for i in range(NT):
                ins = v.max(top[:, i], lg[:, i])
            step(ins)
            for i in range(NT):
                ins = v.max_index(idx[:, i], top[:, i], lg[:, i])
            step(ins)
            v.tensor_tensor(gwt[:, :, 0:1], top[:, :, 0:1], top[:, :, 1:2], ALU.subtract)
            v.tensor_tensor(gwt[:, :, 1:2], top[:, :, 1:2], top[:, :, 0:1], ALU.subtract).then_inc(gate_dif, 1)

            def write0(k):
                if k == 0:
                    v.wait_ge(gate_sig, 1)
                w = gw2[:, :, k:k + 1].broadcast_to([P, NT, E0])
                if k == 0:
                    step(v.tensor_tensor(combt[:], eq[:], w, ALU.mult))
                else:
                    step(v.tensor_tensor(eq[:], eq[:], w, ALU.mult))
                    step(v.tensor_tensor(combt[:], combt[:], eq[:], ALU.add))

            one_hots(write0)
            v.tensor_copy(comb0[:], combt[:].rearrange("p i e -> p e i")).then_inc(comb_rdy, 1)
            v.wait_ge(comb_rdy, 1)

            def invert(u, k):
                v.wait_ge(sd_rdy, u + 5)
                v.reciprocal(inv[:, k % 2], sd[:, k % 4]).then_inc(inv_rdy, 1)

            def coefficients(u, e, k):
                hf = k % 2
                v.wait_ge(inv_rdy, u + 1)
                v.tensor_tensor(coef[:, k % 2], inv[:, k % 2],
                                comb0[:, bass.ds(e, 1), hf * HT:(hf + 1) * HT].rearrange("p a i -> p (a i)"),
                                ALU.mult).then_inc(cf_rdy, 1)

            def weigh(u, e, k):
                v.wait_ge(cf_rdy, u + 1)
                v.wait_ge(added, u + 1)
                for i in range(HT):
                    ins = v.scalar_tensor_tensor(uu[:, k % 2, i], bank[k % 4][:, i * D:(i + 1) * D],
                                                 coef[:, k % 2, i:i + 1],
                                                 m0_gamma[:, bass.ds(e, 1)].rearrange("p a d -> p (a d)"),
                                                 ALU.mult, ALU.mult)
                ins.then_inc(u_rdy, 1)

            def m0_body(j, tail):
                for k in range(M0_UNITS):
                    u = M0_UNITS * j + k
                    if tail and k == 0:
                        for hf in range(HALVES):
                            v.wait_ge(gT_mm, hf + 1)
                            v.tensor_copy(gT[:, hf], bank[6 + hf][0:E0, :]).then_inc(gT_ev, 1)
                    invert(u, k)
                    coefficients(u, 2 * j + k // 2, k)
                    weigh(u, 2 * j + k // 2, k)
                    if tail and k == 3:
                        normalise(4, 0)
                    if tail and k >= 2:
                        hf = k - 2
                        v.wait_ge(beta_add, hf + 1)
                        v.wait_ge(u_rdy, u + 5)
                        v.tensor_tensor(half(h, hf), half(h, hf), uu[:, k % 2], ALU.add).then_inc(last_added, 1)
                        v.wait_ge(last_added, hf + 1)
                        if hf:
                            low_part(4, 0)
                        half_stats(hf)

            with v.Fori(0, E0 // 2 - 1) as j:
                m0_body(j, False)
            m0_body(E0 // 2 - 1, True)

            def query_constants(hf):
                v.wait_ge(small_ev, 1)
                v.wait_ge(r_mm, hf + 1)
                v.tensor_tensor(rr[:], v3(bank[6][:, 0:HT * NH], NH),
                                att_small[:, 2 * NH:3 * NH].unsqueeze(1).broadcast_to([P, HT, NH]),
                                ALU.add).then_inc(r_ev, 1)
                v.wait_ge(r_ev, hf + 1)

            def less_maximum(hf, tp):
                m = 2 * hf + tp
                v.wait_ge(s_mm, m + 1)
                v.transpose(sq_[:, tp].rearrange("p n b -> p (n b)"), bank[2 + tp][:]).then_inc(s_ev, 1)
                v.wait_ge(s_ev, m + 1)
                step(v.tensor_reduce(row[:, 0], sq_[:, tp], AX.X, ALU.max))
                r = rr[:, 2 * tp:2 * tp + 2].rearrange("p i n -> p (i n)")
                step(v.tensor_tensor(row[:, 0], row[:, 0], r, ALU.add))
                step(v.tensor_tensor(row[:, 1], row[:, 0], r, ALU.subtract))
                v.tensor_tensor(sq_[:, tp], sq_[:, tp], row[:, 1].unsqueeze(2).broadcast_to([P, 2 * NH, BLK]),
                                ALU.subtract).then_inc(s_sub, 1)

            def probabilities(hf, tp):
                m = 2 * hf + tp
                v.wait_ge(s_exp, m + 1)
                step(v.tensor_reduce(row[:, 2], sq_[:, tp], AX.X, ALU.add))
                step(v.reciprocal(row[:, 3], row[:, 2]))
                step(v.tensor_tensor(sq_[:, tp], sq_[:, tp], row[:, 3].unsqueeze(2).broadcast_to([P, 2 * NH, BLK]),
                                     ALU.mult))
                if hf:
                    v.wait_ge(px_rdy, 4 * (tp + 1))
                v.transpose(pT[:, tp].rearrange("p n b -> p (n b)"),
                            sq_[:, tp].rearrange("p n b -> p (n b)")).then_inc(pt_rdy, 1)

            normalise(5, 1)
            low_part(5, 1)
            query_constants(0)
            less_maximum(0, 0)
            less_maximum(0, 1)
            probabilities(0, 0)
            probabilities(0, 1)
            query_constants(1)
            less_maximum(1, 0)
            less_maximum(1, 1)
            probabilities(1, 0)
            probabilities(1, 1)
            residual(0, [bank[6], bank[6]], av_mm, 2, av_hb, av_ev)
            normalise(6, 0)
            low_part(6, 0)
            residual(1, [bank[2], bank[6]], av_mm, 2, av_hb, av_ev)
            normalise(7, 1)

            def gated(u, k):
                for c in range(2):
                    q, r = 2 * u + c, (2 * k + c) % 3
                    v.wait_ge(silu_rdy, q + 1)
                    v.wait_ge(b_mm, q + 13)
                    if c == 0:
                        v.wait_ge(y1_mm, u + 1)
                    v.tensor_tensor(hid1[:, k % 2, c], sa[:, r], bank[3 + r][:], ALU.mult).then_inc(hid1_rdy, 1)

            def accumulate(u, e, k):
                hf = k % 2
                v.wait_ge(y1_mm, u + 3)
                v.wait_ge(acc_rdy, u + 1)
                for i in range(HT):
                    ti = hf * HT + i
                    ins = v.scalar_tensor_tensor(h[:, ti], bank[6 + k % 2][:, i * D:(i + 1) * D],
                                                 comb1[:, bass.ds(e, 1), ti:ti + 1].rearrange("p a i -> p (a i)"),
                                                 h[:, ti], ALU.mult, ALU.add)
                ins.then_inc(acc_rdy, 1)

            step(v.memset(comb1[:, 0], 1.0))
            gated(0, 0)
            low_part(7, 1)
            gated(1, 1)
            v.wait_ge(gate_mm, 2)
            v.tensor_copy(lg[:], v3(bank[7][:, 0:NT * E0], E0)).then_inc(gate_ev, 1)
            v.wait_ge(gate_ev, 2)
            step(v.tensor_tensor(lgb[:], lg[:], m1_bias[:].unsqueeze(1).broadcast_to([P, NT, E0]), ALU.add))
            for i in range(NT):
                ins = v.max(top[:, i], lg[:, i])
            step(ins)
            v.tensor_copy(gwt[:], top[:, :, 0:2]).then_inc(gate_dif, 1)
            for i in range(NT):
                ins = v.max(topb[:, i], lgb[:, i])
            step(ins)
            for i in range(NT):
                ins = v.max_index(idx[:, i], topb[:, i], lgb[:, i])
            step(ins)
            v.wait_ge(gate_sig, 2)
            step(v.tensor_scalar(gw2[:], gw2[:], 1.0, None, ALU.add))
            step(v.reciprocal(gw2[:], gw2[:]))
            step(v.tensor_reduce(row[:, 0, 0:NT], gw2[:], AX.X, ALU.add))
            step(v.reciprocal(row[:, 1, 0:NT], row[:, 0, 0:NT]))
            step(v.tensor_tensor(gw2[:], gw2[:], row[:, 1, 0:NT].unsqueeze(2).broadcast_to([P, NT, 2]), ALU.mult))

            def write1(k):
                w = gw2[:, :, k:k + 1].broadcast_to([P, NT, E0])
                if k == 0:
                    step(v.tensor_tensor(lg[:], eq[:], w, ALU.mult))
                else:
                    step(v.tensor_tensor(eq[:], eq[:], w, ALU.mult))
                    step(v.tensor_tensor(comb1[:, 1:E1], lg[:].rearrange("p i e -> p e i"),
                                         eq[:].rearrange("p i e -> p e i"), ALU.add))

            one_hots(write1)

            def m1_body(j, tail):
                for k in range(M1_UNITS):
                    u = M1_UNITS * j + k
                    accumulate(u, 3 * j + k // 2, k)
                    if not tail or k + 2 < M1_UNITS:
                        gated(u + 2, k + 2)

            with v.Fori(0, E1 // 3 - 1) as j:
                m1_body(j, False)
            m1_body(E1 // 3 - 1, True)


def kernel(**inputs):
    import numpy as np
    import concourse.bacc as bacc
    from concourse.bass_utils import run_bass_kernel_spmd

    a = {k: np.asarray(v) for k, v in inputs.items()}
    B = a["x"].shape[0]
    x = a["x"].reshape(B, 3, 4, 16, 4, 16).transpose(1, 3, 5, 0, 2, 4).reshape(KC, P, NT, P).transpose(2, 1, 0, 3)
    host = {
        "x": x,
        "tok_w": a["L0_tok_W"].T.reshape(KC, P, D).transpose(1, 0, 2),
        "tok_b": a["L0_tok_b"],
        "gru_w": a["L0_attn_W_in"].T,
        "gru_b": a["L0_attn_b_in"].reshape(4, P).T,
        "gru_wo": a["L0_attn_W_out"].T.reshape(HG, P, D).transpose(1, 0, 2),
        "gru_bo": a["L0_attn_b_out"],
        "wqT": a["L1_attn_Wq"].transpose(2, 0, 1),
        "wkT": a["L1_attn_Wk"].transpose(2, 0, 1),
        "wvT": a["L1_attn_Wv"].transpose(2, 0, 1),
        "wo": a["L1_attn_Wo"].reshape(NH, P, D).transpose(1, 0, 2),
        "att_b": np.stack([a["L1_attn_bq"], a["L1_attn_bk"], a["L1_attn_bv"]]).transpose(2, 0, 1),
        "m0_gate": a["L0_ffn_Wg"],
        "m0_w1": a["L0_ffn_W1"].transpose(1, 0, 2),
        "m0_b1": a["L0_ffn_b1"].T,
        "m0_w2": a["L0_ffn_W2"].transpose(1, 0, 2),
        "m0_b2": a["L0_ffn_b2"],
        "m0_gamma": a["L0_ffn_gamma"],
        "m0_beta": a["L0_ffn_beta"],
        "m1_gate": a["L1_ffn_gate_w"].T,
        "m1_bias": a["L1_ffn_biases"],
        "m1_w13": np.concatenate([np.concatenate([a["L1_ffn_sw1"][None], a["L1_ffn_w1"]]),
                                  np.concatenate([a["L1_ffn_sw3"][None], a["L1_ffn_w3"]])],
                                 axis=2).transpose(1, 0, 2).reshape(D, E1, 4, P),
        "m1_w2": np.concatenate([a["L1_ffn_sw2"][None], a["L1_ffn_w2"]]).reshape(E1, 2, P, D).transpose(2, 0, 1, 3),
    }
    nc = bacc.Bacc("TRN2", target_bir_lowering=False, num_devices=1)
    arrays, aps = {}, {}
    for name, value in host.items():
        arrays[f"in_{name}"] = np.ascontiguousarray(value)
        aps[name] = nc.dram_tensor(f"in_{name}", arrays[f"in_{name}"].shape, mybir.dt.float32, kind="ExternalInput").ap()
    out = nc.dram_tensor("out", (TOK, D), mybir.dt.float32, kind="ExternalOutput").ap()
    build(nc, aps, out)
    r = run_bass_kernel_spmd(nc, [arrays], core_ids=[0])
    return r.results[0]["out"].reshape(B, SEQ, D)
```

```python
import concourse.bass as bass
from concourse import mybir
from contextlib import ExitStack

ALU = mybir.AluOpType
ACT = mybir.ActivationFunctionType
AX = mybir.AxisListType
F32 = mybir.dt.float32
F32R = mybir.dt.float32r
BF16 = mybir.dt.bfloat16
U32 = mybir.dt.uint32
I32 = mybir.dt.int32

P = 128
D = 128
TOK = 1024
NT = TOK // P
HALVES = 2
HT = NT // HALVES
HC = HT * P
SEQ = 16
KC = 6
HG = 2
E0 = 8
E1 = 9
NH = 8
EPS = 1e-5
SCALE = float(D) ** -0.5
MASKED = -1e30
BLK = 32
LOW = 32
B2_ROWS = 2 * LOW


def build(nc, t, out):
    with ExitStack() as ctx:
        def sb(name, shape, dt=F32):
            return ctx.enter_context(nc.sbuf_tensor(name, shape, dt))

        def sem(name):
            return ctx.enter_context(nc.semaphore(name))

        bank = [ctx.enter_context(nc.psum_tensor(f"bank{i}", [P, 512], F32)) for i in range(8)]

        x_in = sb("x_in", [P, NT, KC, P])
        x_place = x_in[:, :, :, :].rearrange("p i c k -> p (i c k)")
        tok_w = sb("tok_w", [P, KC, D])
        tok_b = sb("tok_b", [P, D])
        gru_w = sb("gru_w", [P, 4 * P])
        gru_b = sb("gru_b", [P, 4])
        gru_wo = sb("gru_wo", [P, HG, D])
        gru_bo = sb("gru_bo", [P, D])
        att_w = sb("att_w", [P, 4, NH, D])
        wkT, wvT, wo, wqT = (att_w[:, i] for i in range(4))
        att_b = sb("att_b", [P, 3, NH])
        m0_gate = sb("m0_gate", [P, E0])
        m0_w1 = sb("m0_w1", [P, E0, P])
        m0_b1 = sb("m0_b1", [P, E0])
        m0_w2 = sb("m0_w2", [P, E0, D])
        m0_b2 = sb("m0_b2", [B2_ROWS, D])
        m0_gamma = sb("m0_gamma", [P, E0, D])
        m0_beta = sb("m0_beta", [E0, D])
        m1_gate = sb("m1_gate", [P, E0])
        m1_bias = sb("m1_bias", [P, E0])
        m1_w13 = sb("m1_w13", [P, E1, 4, P])
        m1_w2 = sb("m1_w2", [P, E1, 2, D])

        ident = sb("ident", [P, P])
        ones = sb("ones", [P, P])
        ones_r = sb("ones_r", [B2_ROWS, P], F32R)
        pick = sb("pick", [B2_ROWS, E0])
        expo = sb("expo", [P, HT])
        own_img = sb("own_img", [P, BLK], BF16)
        other_img = sb("other_img", [P, BLK], BF16)
        iota_i = sb("iota_i", [P, NT, E0], I32)
        iota8 = sb("iota8", [P, NT, E0])
        eps_c = sb("eps_c", [P, 1])
        zero = sb("zero", [P, 1])

        gruH = sb("gruH", [P, 4 * P], F32R)
        gruL = sb("gruL", [P, 4 * P], F32R)
        gru_bn = sb("gru_bn", [P, HG])
        gru_bh = sb("gru_bh", [P, HG])
        GH = sb("GH", [P, NH, D], F32R)
        GL = sb("GL", [P, NH, D], F32R)
        UH = sb("UH", [P, NH, D], F32R)
        UL = sb("UL", [P, NH, D], F32R)
        bqk = sb("bqk", [P, NH])
        att_small = sb("att_small", [P, 3 * NH])
        att_ob = sb("att_ob", [P, D])
        w1H = sb("w1H", [P, 3, P], F32R)
        w1L = sb("w1L", [P, 3, P], F32R)
        w2_mean = sb("w2_mean", [P, E0])
        w2c = sb("w2c", [P, E0, D])
        b2_mean = sb("b2_mean", [B2_ROWS, 1])
        b2c = sb("b2c", [B2_ROWS, D])
        b2H = sb("b2H", [B2_ROWS, D], F32R)
        b2p = sb("b2p", [B2_ROWS, D])
        b2x = sb("b2x", [B2_ROWS, E0, D], F32R)
        w13H = sb("w13H", [P, 3, 4, P], F32R)
        w13L = sb("w13L", [P, 3, 4, P], F32R)

        h = sb("h", [P, NT, D])
        hb = sb("hb", [P, NT, D])
        stats = sb("stats", [P, NT, 6])
        mv = sb("mv", [P, NT, 2])
        ve = sb("ve", [P, NT])
        rstd = sb("rstd", [P, NT])
        xn = sb("xn", [P, HALVES, HT, D])
        xT = sb("xT", [P, TOK])
        xH = sb("xH", [P, TOK], F32R)
        xL = sb("xL", [P, TOK], F32R)
        gru = sb("gru", [P, 4 * HG, HC])
        gf = gru[:, 0:HG]
        gz = gru[:, HG:2 * HG]
        gs = gru[:, 2 * HG:3 * HG]
        gh = [gru[:, 3 * HG:4 * HG], x_place[:, 0:HG * HC].rearrange("p (a c) -> p a c", c=HC)]
        qT = att_w[:, :, :, :].rearrange("p a n d -> p (a n d)").rearrange("p (n c) -> p n c", c=HC)
        V = x_place[:, 0:HT * NH * D].rearrange("p (i n d) -> p i n d", n=NH, d=D)
        rr = sb("rr", [P, HT, NH])
        pT = sb("pT", [P, 2, 2 * NH, BLK])
        score_q = sb("score_q", [P, 2, 2 * NH, BLK])
        row = sb("row", [P, 4, 2 * NH])
        px_place = [x_place[:, 8 * HC:12 * HC], gru[:, 0:4].rearrange("p a c -> p (a c)"),
                    gru[:, 4:8].rearrange("p a c -> p (a c)")]
        px_place = px_place + px_place[0:1]
        PX = [px_place[i // 2].rearrange("p (a n q) -> p a n q", a=2, q=P)[:, i % 2] for i in range(NT)]
        lg = sb("lg", [P, NT, E0])
        lgb = sb("lgb", [P, NT, E0])
        top = sb("top", [P, NT, 8])
        topb = sb("topb", [P, NT, 8])
        idx = sb("idx", [P, NT, 8], U32)
        idf = sb("idf", [P, NT, 2])
        gw2 = sb("gw2", [P, NT, 2])
        gwt = sb("gwt", [P, NT, 2])
        eq = sb("eq", [P, NT, E0])
        comb0 = sb("comb0", [P, E0, NT])
        comb1 = sb("comb1", [P, E1, NT])
        combt = sb("combt", [P, NT, E0])
        hid0 = x_place[:, 0:2 * HC].rearrange("p (a c) -> p a c", c=HC)
        gT = x_place[0:E0, 2 * HC:4 * HC].rearrange("p (a c) -> p a c", c=HC)
        uu = x_place[:, 4 * HC:6 * HC].rearrange("p (a i d) -> p a i d", a=2, d=D)
        der_all = [x_place[:, (2 + i) * HC:(3 + i) * HC].rearrange("p (a d) -> p a d", d=D) for i in range(4)]
        sqy = sb("sqy", [P, HT, D])
        ss = sb("ss", [P, 4, HT])
        sd = sb("sd", [P, 4, HT])
        coef = sb("coef", [P, 2, HT])
        inv = sb("inv", [P, 2, HT])
        hid1 = gru[:, 0:4].rearrange("p (a b) c -> p a b c", b=2)
        sa = gru[:, 4:7]

        x_ld = [sem(f"x_ld{i}") for i in range(NT)]
        tok_ld = sem("tok_ld")
        tok_b_ld = sem("tok_b_ld")
        gru_w_ld = sem("gru_w_ld")
        gru_b_ld = sem("gru_b_ld")
        gru_o_ld = sem("gru_o_ld")
        att_qk_ld = sem("att_qk_ld")
        att_vo_ld = sem("att_vo_ld")
        m0_b2_ld = sem("m0_b2_ld")
        b2_zero = sem("b2_zero")
        m0_ld = sem("m0_ld")
        m1_ld = sem("m1_ld")
        consts = sem("consts")
        pool_step = sem("pool_step")
        dve_step = sem("dve_step")
        act_step = sem("act_step")
        tok_mm = sem("tok_mm")
        tok_ev = sem("tok_ev")
        ln_var = sem("ln_var")
        ln_rstd = sem("ln_rstd")
        xn_rdy = sem("xn_rdy")
        xt_mm = sem("xt_mm")
        xh_rdy = sem("xh_rdy")
        xl_rdy = sem("xl_rdy")
        xt_rdy = sem("xt_rdy")
        gru_split = sem("gru_split")
        gru_mm = sem("gru_mm")
        gru_sig = sem("gru_sig")
        gru_cand = sem("gru_cand")
        gru_scan = sem("gru_scan")
        gru_hb = sem("gru_hb")
        gru_out = sem("gru_out")
        gru_ev = sem("gru_ev")
        der_mm = sem("der_mm")
        der_hi = sem("der_hi")
        der_lo = sem("der_lo")
        small_mm = sem("small_mm")
        small_ev = sem("small_ev")
        bqk_rdy = sem("bqk_rdy")
        b2_parts = sem("b2_parts")
        b2x_rdy = sem("b2x_rdy")
        w2c_rdy = sem("w2c_rdy")
        gate_mm = sem("gate_mm")
        gate_ev = sem("gate_ev")
        gate_dif = sem("gate_dif")
        gate_sig = sem("gate_sig")
        comb_rdy = sem("comb_rdy")
        w1_high = sem("w1_high")
        w1_rdy = sem("w1_rdy")
        h_mm = sem("h_mm")
        hid_rdy = sem("hid_rdy")
        y_mm = sem("y_mm")
        ss_rdy = sem("ss_rdy")
        sd_rdy = sem("sd_rdy")
        inv_rdy = sem("inv_rdy")
        cf_rdy = sem("cf_rdy")
        u_rdy = sem("u_rdy")
        added = sem("added")
        last_added = sem("last_added")
        gT_mm = sem("gT_mm")
        gT_ev = sem("gT_ev")
        beta_mm = sem("beta_mm")
        q_mm = sem("q_mm")
        q_ev = sem("q_ev")
        r_mm = sem("r_mm")
        r_ev = sem("r_ev")
        s_mm = sem("s_mm")
        s_ev = sem("s_ev")
        s_sub = sem("s_sub")
        s_exp = sem("s_exp")
        pt_rdy = sem("pt_rdy")
        px_rdy = sem("px_rdy")
        px_zero = sem("px_zero")
        v_mm = sem("v_mm")
        v_ev = sem("v_ev")
        av_mm = sem("av_mm")
        av_hb = sem("av_hb")
        av_ev = sem("av_ev")
        w13_rdy = sem("w13_rdy")
        a_mm = sem("a_mm")
        b_mm = sem("b_mm")
        silu_rdy = sem("silu_rdy")
        hid1_rdy = sem("hid1_rdy")
        y1_mm = sem("y1_mm")
        y1_two = sem("y1_two")
        acc_rdy = sem("acc_rdy")
        acc_two = sem("acc_two")
        out_st = sem("out_st")
        past = sem("past")

        blk = ctx.enter_context(nc.Block())

        def half(a, hf):
            return a[:, hf * HT:(hf + 1) * HT]

        def cols(hf):
            return slice(hf * HC, (hf + 1) * HC)

        def v3(ap, n):
            return ap.rearrange("p (a b) -> p a b", b=n)

        M0_LOADS, M1_LOADS = 6, 4
        DERIVED = 4
        BETA = bank[6], bank[1]
        Q_BANKS, V_BANKS = (0, 5, 1), (4, 5, 0, 1)
        M0_UNITS, M1_UNITS = 4, 6

        def m0_unit(j, k):
            if isinstance(j, int) and j + k // M0_UNITS == E0 // 2 - 1:
                return E0 - 2 + k % 2, k % M0_UNITS // 2
            return 2 * j + k // 2, k % 2

        def y1(k, i, last):
            return bank[0 if last and i >= 2 else 6 + k % 2]

        @blk.sync
        def _(sp):
            sp.dma_start(tok_w[:], t["tok_w"]).then_inc(tok_ld, 16)
            for i in range(NT):
                sp.dma_start(x_in[:, i], t["x"][i]).then_inc(x_ld[i], 16)
                if i == 1:
                    sp.dma_start(gru_w[:], t["gru_w"]).then_inc(gru_w_ld, 16)
            for dst, name in ((wqT, "wqT"), (wkT, "wkT")):
                sp.dma_start(dst, t[name]).then_inc(att_qk_ld, 16)
            sp.dma_start(gru_wo[:], t["gru_wo"]).then_inc(gru_o_ld, 16)
            for dst, name in ((wvT, "wvT"), (wo, "wo")):
                sp.dma_start(dst, t[name]).then_inc(att_vo_ld, 16)
            for dst, name in ((m0_w1, "m0_w1"), (m0_w2, "m0_w2")):
                sp.dma_start(dst[:], t[name]).then_inc(m0_ld, 16)
            sp.dma_start(m0_gamma[:], t["m0_gamma"].unsqueeze(0).broadcast_to([P, E0, D])).then_inc(m0_ld, 16)
            for dst, name in ((m1_w13, "m1_w13"), (m1_w2, "m1_w2")):
                sp.dma_start(dst[:], t[name]).then_inc(m1_ld, 16)

            def store(i0, i1):
                sp.dma_start(out[i0 * P:i1 * P, :].rearrange("(i p) d -> p i d", p=P),
                             h[:, i0:i1]).then_inc(out_st, 16)

            sp.wait_ge(acc_rdy, 2 + 2 * E1 - 1)
            store(0, HT)
            sp.wait_ge(acc_two, 1)
            store(HT, HT + 2)
            sp.wait_ge(acc_rdy, 2 + 2 * E1)
            store(HT + 2, NT)
            sp.wait_ge(out_st, 16 * 3)

        @blk.gpsimd
        def _(g):
            steps = [0]

            def step(ins):
                steps[0] += 1
                ins.then_inc(pool_step, 1)
                g.wait_ge(pool_step, steps[0])

            g.sem_inc(added, 2)
            g.memset(m0_b2[:], 0.0).then_inc(b2_zero, 1)
            step(g.memset(ident[:], 0.0))
            step(g.affine_select(out=ident[:], in_=ident[:], compare_op=ALU.not_equal, fill=1.0, base=0,
                                 pattern=[[-1, P]], channel_multiplier=1))
            g.memset(expo[:], -0.5)
            g.memset(zero[:], 0.0)
            g.memset(eps_c[:], EPS)
            step(g.memset(ones[:], 1.0))
            step(g.tensor_copy(ones_r[:], ones[0:B2_ROWS, :]))
            g.memset(own_img[:], 0.0)
            step(g.memset(other_img[:], 0.0))
            first, second = slice(0, SEQ), slice(SEQ, BLK)
            for at, own, other in ((0, first, second), (LOW, second, first)):
                step(g.memset(own_img[at:at + 1, own], 1.0))
                step(g.memset(other_img[at:at + 1, other], MASKED))
            step(g.iota(iota_i[:], pattern=[[0, NT], [1, E0]], base=0, channel_multiplier=0))
            g.tensor_copy(iota8[:], iota_i[:]).then_inc(consts, 1)
            g.wait_ge(gru_w_ld, 16)
            step(g.tensor_tensor(gruH[:], gru_w[:], zero[:].broadcast_to([P, 4 * P]), ALU.add))
            g.tensor_tensor(gruL[:], gru_w[:], gruH[:].bitcast(F32), ALU.subtract).then_inc(gru_split, 1)

            def root(n, hf):
                g.wait_ge(ln_var, n + 1)
                g.tensor_tensor(half(rstd, hf), half(ve, hf), expo[:], ALU.pow).then_inc(ln_rstd, 1)

            def gru_bias(hf):
                g.wait_ge(gru_o_ld, 32)
                g.wait_ge(tok_ev, HT * (hf + 1))
                g.tensor_tensor(half(hb, hf), half(h, hf), gru_bo[:].unsqueeze(1).broadcast_to([P, HT, D]),
                                ALU.add).then_inc(gru_hb, 1)

            root(0, 0)
            root(1, 1)
            gru_bias(0)
            gru_bias(1)
            g.wait_ge(tok_mm, NT)
            g.memset(px_place[0], 0.0)

            def derived_low(i, high, low):
                g.wait_ge(der_hi, i + 1)
                g.tensor_tensor(low, der_all[i], high.bitcast(F32), ALU.subtract).then_inc(der_lo, 1)

            derived_low(0, GH[:, 0:4], GL[:, 0:4])
            derived_low(1, GH[:, 4:8], GL[:, 4:8])
            root(2, 0)
            g.wait_ge(b2_parts, 1)
            g.tensor_tensor(b2x[:], b2p[:].unsqueeze(1).broadcast_to([B2_ROWS, E0, D]),
                            pick[:].unsqueeze(2).broadcast_to([B2_ROWS, E0, D]), ALU.mult).then_inc(b2x_rdy, 1)

            def split_w1(e, slot):
                if slot < 2:
                    g.wait_ge(h_mm, 2 * e + 2)
                g.sem_inc(past, 1)
                g.tensor_tensor(w1H[:, slot], m0_w1[:, bass.ds(e, 1)].rearrange("p a n -> p (a n)"),
                                zero[:].broadcast_to([P, P]), ALU.add).then_inc(w1_high, 1)
                g.wait_ge(w1_high, e + 1)
                g.sem_inc(past, 1)
                g.tensor_tensor(w1L[:, slot], m0_w1[:, bass.ds(e, 1)].rearrange("p a n -> p (a n)"),
                                w1H[:, slot].bitcast(F32), ALU.subtract).then_inc(w1_rdy, 1)

            g.wait_ge(m0_ld, 16 * M0_LOADS)
            split_w1(0, 0)
            root(3, 1)
            split_w1(1, 1)
            derived_low(2, UH[:, 0:4], UL[:, 0:4])
            derived_low(3, UH[:, 4:8], UL[:, 4:8])
            g.wait_ge(gru_out, 4)
            step(g.memset(px_place[1], 0.0))
            g.memset(px_place[2], 0.0).then_inc(px_zero, 1)
            split_w1(2, 0)

            def add_unit(u, j, k, before):
                hf = m0_unit(j, k)[1]
                g.wait_ge(u_rdy, u + 5)
                g.wait_ge(added, before)
                g.tensor_tensor(half(h, hf), half(h, hf), uu[:, k % 2], ALU.add).then_inc(added, 1)

            def m0_body(j, more):
                for k in range(M0_UNITS):
                    u = M0_UNITS * j + k
                    if k == 1 and more:
                        split_w1(2 * j + 3, 1)
                    if k == 0 and not more:
                        split_w1(E0 - 1, 2)
                    if k == 3 and more:
                        split_w1(2 * j + 4, 0)
                    add_unit(u, j, k, u + 1)

            with g.Fori(0, E0 // 2 - 2) as j:
                m0_body(j, True)
            m0_body(E0 // 2 - 2, False)
            add_unit(2 * E0 - 4, E0 // 2 - 1, 0, 2 * E0 - 3)
            root(4, 0)
            add_unit(2 * E0 - 2, E0 // 2 - 1, 2, 2 * E0 - 2)
            root(5, 1)

            def split_w13(e, slot):
                g.wait_ge(b_mm, 4 * e + 4)
                g.sem_inc(past, 1)
                src = m1_w13[:, bass.ds(e, 1)].rearrange("p a c n -> p (a c n)")
                high = w13H[:, slot].rearrange("p c n -> p (c n)")
                low = w13L[:, slot].rearrange("p c n -> p (c n)")
                g.tensor_tensor(high, src, zero[:].broadcast_to([P, 4 * P]), ALU.add).then_inc(w13_rdy, 1)
                g.wait_ge(w13_rdy, 2 * e + 1)
                g.sem_inc(past, 1)
                g.tensor_tensor(low, src, high.bitcast(F32), ALU.subtract).then_inc(w13_rdy, 1)

            def att_bias(hf):
                g.wait_ge(last_added, 2 * hf + 2)
                g.wait_ge(small_ev, 1)
                g.tensor_tensor(half(hb, hf), half(h, hf), att_ob[:].unsqueeze(1).broadcast_to([P, HT, D]),
                                ALU.add).then_inc(av_hb, 1)

            att_bias(0)
            att_bias(1)
            g.wait_ge(m1_ld, 16 * M1_LOADS)
            for e in range(3):
                split_w13(e, e)
            root(6, 0)
            root(7, 1)
            with g.Fori(1, E1 // 3) as j:
                for k in range(3):
                    split_w13(3 * j + k, k)

        @blk.scalar
        def _(act):
            act.sem_inc(hid_rdy, 2)
            act.sem_inc(sd_rdy, 4)
            act.dma_start(gru_b[:], t["gru_b"]).then_inc(gru_b_ld, 16)
            act.dma_start(tok_b[:], t["tok_b"].unsqueeze(0).broadcast_to([P, D])).then_inc(tok_b_ld, 16)
            act.dma_start(gru_bo[:], t["gru_bo"].unsqueeze(0).broadcast_to([P, D])).then_inc(gru_o_ld, 16)
            act.dma_start(att_b[:], t["att_b"]).then_inc(att_qk_ld, 16)
            act.wait_ge(b2_zero, 1)
            for row in (0, LOW):
                act.dma_start(m0_b2[row:row + E0, :], t["m0_b2"]).then_inc(m0_b2_ld, 16)
            for dst, name in ((m0_gate, "m0_gate"), (m0_b1, "m0_b1"), (m0_beta, "m0_beta")):
                act.dma_start(dst[:], t[name]).then_inc(m0_ld, 16)
            act.dma_start(m1_gate[:], t["m1_gate"]).then_inc(m1_ld, 16)
            act.dma_start(m1_bias[:], t["m1_bias"].unsqueeze(0).broadcast_to([P, E0])).then_inc(m1_ld, 16)

            def high_part(n, hf):
                act.wait_ge(xt_mm, n + 1)
                act.activation(xH[:, cols(hf)], bank[7][:], ACT.Copy).then_inc(xh_rdy, 1)

            def whole(n, hf):
                act.wait_ge(xl_rdy, n + 1)
                act.activation(xT[:, cols(hf)], bank[7][:], ACT.Copy).then_inc(xt_rdy, 1)

            def gru_sigmoids(hf, c):
                act.wait_ge(gru_mm, HG * hf + c + 1)
                if hf:
                    act.wait_ge(gru_scan, c + 1)
                act.activation(gf[:, c], bank[2 + c][:], ACT.Sigmoid, bias=gru_bn[:, c:c + 1], scale=-1.0)
                act.activation(gz[:, c], bank[2 + c][:], ACT.Sigmoid, bias=gru_b[:, 2 + c:3 + c])
                act.activation(gs[:, c], bank[c][:], ACT.Sigmoid, bias=gru_b[:, c:c + 1]).then_inc(gru_sig, 1)

            def derived_out(i, high):
                act.wait_ge(der_mm, i + 1)
                act.activation(high, v3(bank[5 + i % 2][:], D), ACT.Copy)
                act.activation(der_all[i], v3(bank[5 + i % 2][:], D), ACT.Copy).then_inc(der_hi, 1)

            act.preload_act_table(ACT.Sigmoid)
            high_part(0, 0)
            act.wait_ge(gru_b_ld, 16)
            act.wait_ge(dve_step, 1)
            gru_sigmoids(0, 0)
            high_part(1, 1)
            gru_sigmoids(0, 1)
            derived_out(0, GH[:, 0:4])
            derived_out(1, GH[:, 4:8])
            gru_sigmoids(1, 0)
            gru_sigmoids(1, 1)
            derived_out(2, UH[:, 0:4])
            derived_out(3, UH[:, 4:8])
            act.wait_ge(m0_ld, 16 * M0_LOADS)
            for e in range(E0):
                ins = act.activation(w2c[:, e], m0_w2[:, e], ACT.Copy, scale=-1.0 / D, accum_out=w2_mean[:, e:e + 1])
            ins.then_inc(act_step, 1)
            act.wait_ge(act_step, 1)
            for e in range(E0):
                ins = act.activation(w2c[:, e], m0_w2[:, e], ACT.Identity, bias=w2_mean[:, e:e + 1])
            ins.then_inc(w2c_rdy, 1)
            high_part(2, 0)
            whole(2, 0)

            def relu(u, e, k):
                act.wait_ge(h_mm, u + 5)
                act.wait_ge(y_mm, u + 1)
                act.sem_inc(past, 1)
                act.activation(hid0[:, k % 2], bank[4 + k % 2][:], ACT.Relu,
                               bias=m0_b1[:, bass.ds(e, 1)]).then_inc(hid_rdy, 1)

            def square(u, k, first=False):
                act.wait_ge(y_mm, u + 3)
                if not first:
                    act.wait_ge(ss_rdy, u)
                for i in range(HT):
                    ins = act.activation(sqy[:, i], bank[k % 4][:, i * D:(i + 1) * D], ACT.Square,
                                         accum_out=ss[:, k % 4, i:i + 1])
                ins.then_inc(ss_rdy, 1)

            def deviation(u, k):
                act.wait_ge(ss_rdy, u + 1)
                act.wait_ge(u_rdy, u + 1)
                act.activation(sd[:, k % 4], ss[:, k % 4], ACT.Sqrt, scale=1.0 / D,
                               bias=eps_c[:, 0:1]).then_inc(sd_rdy, 1)

            act.wait_ge(m0_ld, 16 * M0_LOADS)
            relu(0, 0, 0)
            high_part(3, 1)
            square(0, 0, first=True)
            whole(3, 1)
            relu(1, 0, 1)
            relu(2, 1, 2)
            act.wait_ge(gate_dif, 1)
            act.activation(gw2[:], gwt[:], ACT.Sigmoid).then_inc(gate_sig, 1)
            act.preload_act_table(ACT.Sqrt)
            square(1, 1)

            def m0_body(j, tail):
                for k in range(M0_UNITS):
                    u = M0_UNITS * j + k
                    if not tail or k in (0, 3):
                        deviation(u, k)
                    if not tail or k + 3 < M0_UNITS:
                        relu(u + 3, m0_unit(j, k + 3)[0], k + 3)
                    if tail and k == 1:
                        deviation(u, k)
                        deviation(u + 1, k + 1)
                    if not tail or k + 2 < M0_UNITS:
                        square(u + 2, k + 2)

            with act.Fori(0, E0 // 2 - 2) as j:
                m0_body(j, False)
            m0_body(E0 // 2 - 2, False)
            m0_body(E0 // 2 - 1, True)

            def q_out(hf, i):
                act.wait_ge(q_mm, NH * hf + i + 1)
                if i == 0 and hf:
                    act.wait_ge(s_mm, 2)
                act.activation(qT[:, i], bank[Q_BANKS[(NH * hf + i) % 3]][:], ACT.Identity,
                               bias=att_small[:, i:i + 1]).then_inc(q_ev, 1)

            def exps(hf, tp):
                act.wait_ge(s_sub, 2 * hf + tp + 1)
                act.activation(score_q[:, tp], score_q[:, tp], ACT.Exp, scale=SCALE).then_inc(s_exp, 1)

            def spread(hf, tp):
                act.wait_ge(pt_rdy, 2 * hf + tp + 1)
                if hf and tp:
                    act.wait_ge(av_mm, 2)
                two = px_place[2 * hf + tp].rearrange("p (n q) -> p n q", q=P)
                for j in range(4):
                    q = slice(BLK * j, BLK * (j + 1))
                    act.activation(two[q, :, q], pT[q, tp], ACT.Copy).then_inc(px_rdy, 1)

            def v_out(hf, i):
                act.wait_ge(v_mm, 2 * HT * hf + i + 1)
                if hf:
                    act.wait_ge(av_mm, i // 2 + 1)
                act.activation(V[:, i // 2, 4 * (i % 2):4 * (i % 2) + 4], v3(bank[V_BANKS[i % 4]][:], D),
                               ACT.Copy).then_inc(v_ev, 1)

            act.preload_act_table(ACT.Exp)
            act.wait_ge(small_mm, 1)
            act.activation(att_small[:, 0:NH], bank[4][:, 0:NH], ACT.Copy)
            act.activation(att_ob[:], bank[4][:, P:2 * P], ACT.Copy).then_inc(small_ev, 1)
            high_part(4, 0)
            act.wait_ge(small_ev, 1)
            q_out(0, 0)
            whole(4, 0)
            for i in range(1, NH // 2):
                q_out(0, i)
            high_part(5, 1)
            q_out(0, 4)
            whole(5, 1)
            q_out(0, 5)
            act.wait_ge(small_mm, 2)
            act.activation(att_small[:, NH:3 * NH], bank[4][:, NH:3 * NH], ACT.Copy).then_inc(small_ev, 1)
            q_out(0, 6)
            q_out(0, 7)
            for i in range(NH):
                if i in (NH // 2, NH - 1):
                    exps(0, i // (NH - 1))
                q_out(1, i)
            act.wait_ge(px_zero, 1)
            for i in range(2 * HT):
                if i == 2:
                    spread(0, 0)
                    spread(0, 1)
                if i == 5:
                    exps(1, 0)
                v_out(0, i)
            exps(1, 1)
            spread(1, 0)
            spread(1, 1)
            for i in range(2 * HT):
                v_out(1, i)
            high_part(6, 0)
            whole(6, 0)

            def silu(q, k):
                act.wait_ge(a_mm, q + 1)
                act.wait_ge(hid1_rdy, q + 1)
                act.activation(sa[:, k % 3], bank[k % 3][:], ACT.Silu).then_inc(silu_rdy, 1)

            silu(0, 0)
            silu(1, 1)
            high_part(7, 1)
            whole(7, 1)
            silu(2, 2)
            silu(3, 3)
            act.wait_ge(gate_dif, 2)
            act.activation(gw2[:], gwt[:], ACT.Exp, scale=-1.0).then_inc(gate_sig, 1)
            act.preload_act_table(ACT.Silu)

            AHEAD = 4

            def m1_body(j, tail):
                for k in range(2 * M1_UNITS - (AHEAD if tail else 0)):
                    silu(2 * M1_UNITS * j + k + AHEAD, k + AHEAD)

            with act.Fori(0, E1 // 3 - 1) as j:
                m1_body(j, False)
            m1_body(E1 // 3 - 1, True)

        @blk.tensor
        def _(pe):
            def three(dst, lh, ll, rh, rl):
                pe.matmul(dst, lh, rh, start=True, stop=False)
                pe.matmul(dst, lh, rl, start=False, stop=False)
                return pe.matmul(dst, ll, rh, start=False, stop=True)

            def transposes(n, hf):
                pe.wait_ge(xn_rdy, n + 1)
                if n:
                    pe.wait_ge(xl_rdy, n)
                if n > 2:
                    pe.wait_ge(xt_rdy, n - 2)
                for i in range(HT):
                    ins = pe.transpose(bank[7][:, i * P:(i + 1) * P], xn[:, hf, i], ident[:])
                ins.then_inc(xt_mm, 1)

            def x_ready(n):
                pe.wait_ge(xl_rdy, n + 1)

            for s, n in ((h_mm, 4), (y_mm, 2), (b_mm, 12), (y1_mm, 2)):
                pe.sem_inc(s, n)
            pe.wait_ge(tok_ld, 16)
            pe.wait_ge(consts, 1)
            for i in range(NT):
                if i == NT - 1:
                    transposes(0, 0)
                pe.wait_ge(x_ld[i], 16)
                if i >= 2:
                    pe.wait_ge(tok_ev, i - 1)
                for c in range(KC):
                    ins = pe.matmul(bank[4 + i % 2][:, 0:D], x_in[:, i, c], tok_w[:, c],
                                    start=c == 0, stop=c == KC - 1)
                ins.then_inc(tok_mm, 1)

            def gru_in(hf):
                x_ready(hf)
                for c in range(HG):
                    if hf:
                        pe.wait_ge(gru_sig, c + 1)
                        pe.wait_ge(gru_cand, c + 1)
                    for b in (c, 2 + c):
                        ins = three(bank[b][:], gruH[:, b * P:(b + 1) * P], gruL[:, b * P:(b + 1) * P],
                                    xH[:, cols(hf)], xL[:, cols(hf)])
                    ins.then_inc(gru_mm, 1)

            def gru_project(hf):
                pe.wait_ge(gru_scan, HG * (hf + 1))
                pe.wait_ge(gru_o_ld, 32)
                for i in range(HT):
                    dst = bank[4][:] if hf == 0 else bank[i // 2][:]
                    for c in range(HG):
                        ins = pe.matmul(dst[:, i * D:(i + 1) * D], gh[hf][:, c, i * P:(i + 1) * P], gru_wo[:, c],
                                        start=c == 0, stop=c == HG - 1)
                    if i % 2:
                        ins.then_inc(gru_out, 1)

            def derive(i, left, right):
                if i >= 2:
                    pe.wait_ge(der_hi, i - 1)
                for k in range(4):
                    n = 4 * (i % 2) + k
                    ins = pe.matmul(bank[5 + i % 2][:, k * D:(k + 1) * D], left[:, n], right[:, n],
                                    start=True, stop=True)
                ins.then_inc(der_mm, 1)

            pe.wait_ge(gru_split, 1)
            gru_in(0)
            transposes(1, 1)
            pe.wait_ge(att_qk_ld, 16 * 3)
            pe.wait_ge(tok_ev, NT)
            derive(0, wqT, wkT)
            derive(1, wqT, wkT)
            gru_in(1)
            gru_project(0)
            pe.wait_ge(att_vo_ld, 16 * 2)
            derive(2, wvT, wo)
            derive(3, wvT, wo)
            gru_project(1)

            def logits(stage, hf, weights):
                pe.wait_ge(xt_rdy, HALVES * 2 * stage + hf + 1)
                for i in range(hf * HT, (hf + 1) * HT):
                    ins = pe.matmul(bank[6 + stage][:, i * E0:(i + 1) * E0], xT[:, i * P:(i + 1) * P], weights[:],
                                    start=True, stop=True)
                if hf:
                    ins.then_inc(gate_mm, 1)

            transposes(2, 0)
            pe.wait_ge(m0_ld, 16 * M0_LOADS)
            def w1_product(u, j, k):
                e, hf = m0_unit(j, k)
                pe.wait_ge(w1_rdy, e + 1)
                pe.wait_ge(hid_rdy, u + 1)
                s = (2 if e == E0 - 1 else e % 2) if isinstance(j, int) else k // 2 % 2
                ins = three(bank[4 + k % 2][:], w1H[:, s], w1L[:, s], xH[:, cols(hf)], xL[:, cols(hf)])
                ins.then_inc(h_mm, 1)

            def w2_product(u, e, k):
                pe.wait_ge(hid_rdy, u + 3)
                pe.wait_ge(u_rdy, u + 1)
                pe.sem_inc(past, 1)
                y = v3(bank[k % 4][:], D)
                pe.matmul(y, ones_r[:], b2x[:, bass.ds(e, 1)].broadcast_to([B2_ROWS, HT, D]),
                          start=True, stop=False, skip_group_check=True)
                for i in range(HT):
                    ins = pe.matmul(bank[k % 4][:, i * D:(i + 1) * D], hid0[:, k % 2, i * P:(i + 1) * P],
                                    w2c[:, bass.ds(e, 1)].rearrange("p a d -> p (a d)"),
                                    start=False, stop=i == HT - 1, skip_group_check=True)
                ins.then_inc(y_mm, 1)

            pe.wait_ge(gru_ev, 2)
            x_ready(2)
            w1_product(0, 0, 0)
            transposes(3, 1)
            pe.wait_ge(w2c_rdy, 1)
            pe.wait_ge(b2x_rdy, 1)
            pe.wait_ge(gru_ev, 4)
            w2_product(0, 0, 0)
            pe.wait_ge(der_hi, 4)
            logits(0, 0, m0_gate)
            x_ready(3)
            w1_product(1, 0, 1)
            logits(0, 1, m0_gate)

            def betas(hf):
                pe.wait_ge(gT_ev, hf + 1)
                if hf:
                    pe.wait_ge(u_rdy, 2 * E0 + 2)
                for i in range(HT):
                    ins = pe.matmul(BETA[hf][:, i * D:(i + 1) * D], gT[:, hf, i * P:(i + 1) * P], m0_beta[:],
                                    start=True, stop=True)
                ins.then_inc(beta_mm, 1)

            def m0_body(j, tail):
                for k in range(M0_UNITS):
                    u = M0_UNITS * j + k
                    if tail and k == 0:
                        pe.wait_ge(comb_rdy, 1)
                        pe.wait_ge(xt_rdy, 2)
                        for i in range(NT):
                            ins = pe.matmul(bank[6 + i // HT][0:E0, i % HT * P:(i % HT + 1) * P],
                                            combt[:, i], ident[:], start=True, stop=True)
                            if i % HT == HT - 1:
                                ins.then_inc(gT_mm, 1)
                    if not tail or k + 2 < M0_UNITS:
                        w1_product(u + 2, j, k + 2)
                    if not tail or k + 1 < M0_UNITS:
                        w2_product(u + 1, m0_unit(j, k + 1)[0], k + 1)
                    if tail and k == 1:
                        betas(0)

            with pe.Fori(0, E0 // 2 - 2) as j:
                m0_body(j, False)
            m0_body(E0 // 2 - 2, False)
            m0_body(E0 // 2 - 1, True)

            def q_project(hf, heads):
                for i in heads:
                    n = NH * hf + i
                    if n >= 3:
                        pe.wait_ge(q_ev, n - 2)
                    three(bank[Q_BANKS[n % 3]][:], GH[:, i], GL[:, i],
                          xH[:, cols(hf)], xL[:, cols(hf)]).then_inc(q_mm, 1)

            def r_project(hf):
                pe.wait_ge(xt_rdy, HALVES + hf + 1)
                pe.wait_ge(small_ev, 2)
                if hf:
                    pe.wait_ge(r_ev, hf)
                for i in range(HT):
                    tok = (hf * HT + i) * P
                    ins = pe.matmul(bank[6][:, i * NH:(i + 1) * NH], xT[:, tok:tok + P], att_small[:, NH:2 * NH],
                                    start=True, stop=True)
                ins.then_inc(r_mm, 1)

            def scores(hf):
                pe.wait_ge(q_ev, NH * (hf + 1))
                for tp in range(2):
                    if hf:
                        pe.wait_ge(s_ev, tp + 1)
                    for i in range(2):
                        for j in range(4):
                            c = (2 * tp + i) * P + BLK * j
                            tok = hf * HC + c
                            ins = pe.matmul(v3(bank[2 + tp][BLK * j:BLK * (j + 1), i * 256:(i + 1) * 256], BLK),
                                            xT[:, tok:tok + BLK], qT[:, :, c:c + BLK], start=True, stop=False,
                                            skip_group_check=True)
                        for j in range(4):
                            ins = pe.matmul(v3(bank[2 + tp][BLK * j:BLK * (j + 1), i * 256:(i + 1) * 256], BLK),
                                            own_img[:], other_img[:].unsqueeze(1).broadcast_to([P, NH, BLK]),
                                            start=False, stop=True, skip_group_check=True)
                    ins.then_inc(s_mm, 1)

            def values(hf, tiles):
                for i in tiles:
                    tok = (hf * HT + i) * P
                    for c in range(2):
                        n = 2 * HT * hf + 2 * i + c
                        if 1 <= n < 4:
                            pe.wait_ge(q_ev, 2 * NH - (2 if n == 1 else 0))
                        if n >= 4:
                            pe.wait_ge(v_ev, n - 3)
                        three(v3(bank[V_BANKS[n % 4]][:], D), xH[:, tok:tok + P], xL[:, tok:tok + P],
                              UH[:, 4 * c:4 * c + 4], UL[:, 4 * c:4 * c + 4]).then_inc(v_mm, 1)

            def attend(hf):
                pe.wait_ge(r_ev, HALVES)
                pe.wait_ge(s_ev, 2 + hf)
                for i in range(HT):
                    pe.wait_ge(v_ev, 2 * (HT * hf + i + 1))
                    if i % 2 == 0:
                        pe.wait_ge(px_rdy, 4 * (2 * hf + i // 2 + 1))
                    if hf and i == 2:
                        pe.wait_ge(av_ev, 2)
                    dst = bank[2 if hf and i < 2 else 6][:]
                    for n in range(NH):
                        ins = pe.matmul(dst[:, i * D:(i + 1) * D], PX[hf * HT + i][:, n], V[:, i, n],
                                        start=n == 0, stop=n == NH - 1)
                    ins.then_inc(av_mm, 1)

            pe.wait_ge(hid_rdy, 2 * E0 + 2)
            for n in range(NH):
                pe.matmul(bank[4][:, n:n + 1], wkT[:, n], att_b[:, 0, n:n + 1], start=True, stop=True)
            for n in range(NH):
                ins = pe.matmul(bank[4][:, P:2 * P], att_b[:, 2, n:n + 1].broadcast_to([P, P]), wo[:, n],
                                start=n == 0, stop=n == NH - 1)
            ins.then_inc(small_mm, 1)
            betas(1)
            transposes(4, 0)
            pe.wait_ge(u_rdy, 2 * E0 + 4)
            x_ready(4)
            pe.wait_ge(der_lo, DERIVED)
            q_project(0, [0, 1])
            pe.wait_ge(last_added, 2 * HALVES)
            q_project(0, [2, 3])
            pe.wait_ge(bqk_rdy, 1)
            pe.wait_ge(small_ev, 1)
            for n in range(NH):
                pe.matmul(bank[4][:, NH + n:NH + n + 1], wqT[:, n], att_b[:, 1, n:n + 1], start=True, stop=True)
            pe.matmul(bank[4][:, 2 * NH:3 * NH], ones[:], bqk[:], start=True, stop=True).then_inc(small_mm, 1)
            transposes(5, 1)
            q_project(0, range(NH // 2, NH))
            r_project(0)
            scores(0)
            x_ready(5)
            r_project(1)
            q_project(1, range(NH))
            values(0, [0])
            scores(1)
            values(0, range(1, HT))
            attend(0)
            values(1, range(HT))
            transposes(6, 0)
            attend(1)

            def w13_products(u, e, k):
                if k % 2 == 0:
                    pe.wait_ge(w13_rdy, 2 * e + 2)
                s = (k // 2) % 3
                for c in range(2):
                    q, r = 2 * u + c, (2 * k + c) % 3
                    pe.wait_ge(hid1_rdy, q + 1)
                    three(bank[r][:], w13H[:, s, c], w13L[:, s, c], xH[:, cols(k % 2)],
                          xL[:, cols(k % 2)]).then_inc(a_mm, 1)
                    ins = three(bank[3 + r][:], w13H[:, s, 2 + c], w13L[:, s, 2 + c], xH[:, cols(k % 2)],
                                xL[:, cols(k % 2)])
                    ins.then_inc(b_mm, 1)

            def w2_products(u, e, k, last=False):
                pe.wait_ge(hid1_rdy, 2 * u + 5)
                pe.wait_ge(acc_rdy, u + 1)
                for i in range(HT):
                    for c in range(2):
                        ins = pe.matmul(y1(k, i, last)[:, i * D:(i + 1) * D], hid1[:, k % 2, c, i * P:(i + 1) * P],
                                        m1_w2[:, bass.ds(e, 1), c].rearrange("p a d -> p (a d)"),
                                        start=c == 0, stop=c == 1)
                    if last and i == 1:
                        ins.then_inc(y1_two, 1)
                ins.then_inc(y1_mm, 1)

            x_ready(6)
            pe.wait_ge(m1_ld, 16 * M1_LOADS)
            pe.wait_ge(v_ev, 4 * HT)
            w13_products(0, 0, 0)
            transposes(7, 1)
            pe.wait_ge(av_ev, 2 * HALVES)
            w2_products(0, 0, 0)
            pe.wait_ge(xt_rdy, 6)
            logits(1, 0, m1_gate)
            logits(1, 1, m1_gate)
            x_ready(7)
            w13_products(1, 0, 1)
            pe.wait_ge(gate_ev, 2)

            def m1_body(j, tail):
                for k in range(M1_UNITS):
                    u = M1_UNITS * j + k
                    if not tail or k + 2 < M1_UNITS:
                        w13_products(u + 2, 3 * j + (k + 2) // 2, k + 2)
                    if not tail or k + 1 < M1_UNITS:
                        w2_products(u + 1, 3 * j + (k + 1) // 2, k + 1, tail and k + 2 == M1_UNITS)

            with pe.Fori(0, E1 // 3 - 1) as j:
                m1_body(j, False)
            m1_body(E1 // 3 - 1, True)

        @blk.vector
        def _(v):
            steps = [0]

            def step(ins):
                steps[0] += 1
                ins.then_inc(dve_step, 1)
                v.wait_ge(dve_step, steps[0])

            def tile_stats(i):
                step(v.bn_stats(stats[:, i], h[:, i]))
                step(v.bn_aggr(mv[:, i], stats[:, i]))

            def variances(hf):
                v.tensor_scalar(half(ve, hf), half(mv, hf)[:, :, 1], EPS, None, ALU.add).then_inc(ln_var, 1)

            def half_stats(hf):
                for i in range(hf * HT, (hf + 1) * HT):
                    ins = v.bn_stats(stats[:, i], h[:, i])
                step(ins)
                for i in range(hf * HT, (hf + 1) * HT):
                    ins = v.bn_aggr(mv[:, i], stats[:, i])
                step(ins)
                variances(hf)

            def normalise(n, hf):
                v.wait_ge(ln_rstd, n + 1)
                if n >= 2:
                    v.wait_ge(xt_mm, n - 1)
                for i in range(HT):
                    ti = hf * HT + i
                    ins = v.tensor_scalar(xn[:, hf, i], h[:, ti], mv[:, ti, 0:1], rstd[:, ti:ti + 1],
                                          ALU.subtract, ALU.mult)
                ins.then_inc(xn_rdy, 1)

            def low_part(n, hf):
                v.wait_ge(xh_rdy, n + 1)
                v.tensor_tensor(xL[:, cols(hf)], bank[7][:], xH[:, cols(hf)].bitcast(F32),
                                ALU.subtract).then_inc(xl_rdy, 1)

            def residual(hf, banks, made, per_two, biased, taken, meanwhile=None):
                for i in range(0, HT, 2):
                    n = (hf * HT + i) // 2
                    tiles = slice(hf * HT + i, hf * HT + i + 2)
                    v.wait_ge(made, per_two * (n + 2 if banks[0] is banks[1] and i == 0 else n + 1))
                    v.wait_ge(biased, hf + 1)
                    v.tensor_tensor(h[:, tiles], v3(banks[i // 2][:, i * D:(i + 2) * D], D), hb[:, tiles],
                                    ALU.add).then_inc(taken, 1)
                    v.wait_ge(taken, n + 1)
                    for k in range(hf * HT + i, hf * HT + i + 2):
                        ins = v.bn_stats(stats[:, k], h[:, k])
                    step(ins)
                    if meanwhile and i == 0:
                        meanwhile()
                for i in range(hf * HT, (hf + 1) * HT):
                    ins = v.bn_aggr(mv[:, i], stats[:, i])
                step(ins)
                variances(hf)

            for s, n in ((u_rdy, 4), (hid1_rdy, 3), (acc_rdy, 2)):
                v.sem_inc(s, n)
            v.wait_ge(gru_b_ld, 16)
            step(v.tensor_scalar(gru_bn[:], gru_b[:, 2:4], -1.0, None, ALU.mult))
            step(v.tensor_scalar(gru_bh[:], gru_b[:, 0:2], 0.5, None, ALU.add))
            v.wait_ge(consts, 1)
            for row0 in (0, LOW):
                ins = v.tensor_copy(pick[row0:row0 + BLK, :], ident[row0:row0 + BLK, row0:row0 + E0])
            step(ins)

            v.wait_ge(tok_b_ld, 16)
            for i in range(NT):
                if i == NT - 1:
                    low_part(0, 0)
                v.wait_ge(tok_mm, i + 1)
                v.tensor_tensor(h[:, i], bank[4 + i % 2][:, 0:D], tok_b[:], ALU.add).then_inc(tok_ev, 1)
                v.wait_ge(tok_ev, i + 1)
                tile_stats(i)
                if i == 1:
                    v.wait_ge(m0_b2_ld, 16 * 2)
                    step(v.tensor_reduce(b2_mean[:], m0_b2[:], AX.X, ALU.add))
                    step(v.tensor_scalar(b2_mean[:], b2_mean[:], 1.0 / D, None, ALU.mult))
                    step(v.tensor_scalar(b2c[:], m0_b2[:], b2_mean[:], None, ALU.subtract))
                    step(v.tensor_copy(b2H[:], b2c[:]))
                    v.tensor_copy(b2p[0:LOW, :], b2H[0:LOW, :].bitcast(F32))
                    v.tensor_tensor(b2p[LOW:2 * LOW, :], b2c[LOW:2 * LOW, :], b2H[LOW:2 * LOW, :].bitcast(F32),
                                    ALU.subtract).then_inc(b2_parts, 1)
                if i == HT - 1:
                    variances(0)
                if i == HT:
                    normalise(0, 0)
                if i == NT - 1:
                    variances(1)
            normalise(1, 1)

            def gru_chunk(hf, c, meanwhile=None):
                k = HG * hf + c
                v.wait_ge(gru_sig, k + 1)
                v.scalar_tensor_tensor(gs[:, c], bank[c][:], gru_bh[:, c:c + 1], gs[:, c],
                                       ALU.add, ALU.max).then_inc(gru_cand, 1)
                if meanwhile:
                    meanwhile()
                v.wait_ge(gru_cand, k + 1)
                v.memset(gf[:, c].rearrange("p (b s) -> p b s", s=SEQ)[:, :, 0:1], 0.0)
                step(v.tensor_tensor(gz[:, c], gz[:, c], gs[:, c], ALU.mult))
                v.tensor_tensor_scan(gh[hf][:, c], gf[:, c], gz[:, c], 0.0, ALU.mult, ALU.add).then_inc(gru_scan, 1)

            gru_chunk(0, 0, lambda: low_part(1, 1))
            gru_chunk(0, 1)
            v.wait_ge(att_qk_ld, 16 * 3)
            v.tensor_tensor(bqk[:], att_b[:, 0], att_b[:, 1], ALU.mult).then_inc(bqk_rdy, 1)
            gru_chunk(1, 0)
            gru_chunk(1, 1)
            residual(0, [bank[4], bank[4]], gru_out, 1, gru_hb, gru_ev)
            residual(1, [bank[0], bank[1]], gru_out, 1, gru_hb, gru_ev, lambda: normalise(2, 0))
            low_part(2, 0)
            normalise(3, 1)

            def one_hots(write):
                step(v.tensor_copy(idf[:], idx[:, :, 0:2]))
                for k in range(2):
                    step(v.tensor_tensor(eq[:], iota8[:], idf[:, :, k:k + 1].broadcast_to([P, NT, E0]), ALU.is_equal))
                    write(k)

            v.wait_ge(der_lo, DERIVED)
            low_part(3, 1)
            v.wait_ge(gate_mm, 1)
            v.tensor_copy(lg[:], v3(bank[6][:, 0:NT * E0], E0)).then_inc(gate_ev, 1)
            v.wait_ge(gate_ev, 1)
            for i in range(NT):
                ins = v.max(top[:, i], lg[:, i])
            step(ins)
            for i in range(NT):
                ins = v.max_index(idx[:, i], top[:, i], lg[:, i])
            step(ins)
            v.tensor_tensor(gwt[:, :, 0:1], top[:, :, 0:1], top[:, :, 1:2], ALU.subtract)
            v.tensor_tensor(gwt[:, :, 1:2], top[:, :, 1:2], top[:, :, 0:1], ALU.subtract).then_inc(gate_dif, 1)

            def write0(k):
                if k == 0:
                    v.wait_ge(gate_sig, 1)
                w = gw2[:, :, k:k + 1].broadcast_to([P, NT, E0])
                if k == 0:
                    step(v.tensor_tensor(combt[:], eq[:], w, ALU.mult))
                else:
                    step(v.tensor_tensor(eq[:], eq[:], w, ALU.mult))
                    step(v.tensor_tensor(combt[:], combt[:], eq[:], ALU.add))

            one_hots(write0)
            v.tensor_copy(comb0[:], combt[:].rearrange("p i e -> p e i")).then_inc(comb_rdy, 1)
            v.wait_ge(comb_rdy, 1)

            def invert(u, k):
                v.wait_ge(sd_rdy, u + 5)
                v.reciprocal(inv[:, k % 2], sd[:, k % 4]).then_inc(inv_rdy, 1)

            def coefficients(u, e, hf, k):
                v.wait_ge(inv_rdy, u + 1)
                v.tensor_tensor(coef[:, k % 2], inv[:, k % 2],
                                comb0[:, bass.ds(e, 1), hf * HT:(hf + 1) * HT].rearrange("p a i -> p (a i)"),
                                ALU.mult).then_inc(cf_rdy, 1)

            def weigh(u, e, k, last=False):
                v.wait_ge(cf_rdy, u + 1)
                if not last:
                    v.wait_ge(added, u + 1)
                for i in range(HT):
                    ins = v.scalar_tensor_tensor(uu[:, k % 2, i], bank[k % 4][:, i * D:(i + 1) * D],
                                                 coef[:, k % 2, i:i + 1],
                                                 m0_gamma[:, bass.ds(e, 1)].rearrange("p a d -> p (a d)"),
                                                 ALU.mult, ALU.mult)
                ins.then_inc(u_rdy, 1)

            def m0_body(j, tail):
                for k in range(M0_UNITS):
                    u = M0_UNITS * j + k
                    if tail and k == 0:
                        for hf in range(HALVES):
                            v.wait_ge(gT_mm, hf + 1)
                            v.tensor_copy(gT[:, hf], bank[6 + hf][0:E0, :]).then_inc(gT_ev, 1)
                    e, hf = m0_unit(j, k)
                    invert(u, k)
                    coefficients(u, e, hf, k)
                    weigh(u, e, k, tail and k == 3)
                    if tail and k == 2:
                        normalise(4, 0)
                    if tail and k == 3:
                        low_part(4, 0)
                    if tail and k % 2:
                        v.wait_ge(added, 2 * E0 - 1 + hf)
                        v.wait_ge(u_rdy, u + 5)
                        v.tensor_tensor(half(h, hf), half(h, hf), uu[:, k % 2], ALU.add).then_inc(last_added, 1)
                        v.wait_ge(last_added, 2 * hf + 1)
                        v.wait_ge(beta_mm, hf + 1)
                        v.tensor_tensor(half(h, hf), half(h, hf), v3(BETA[hf][:], D), ALU.add).then_inc(last_added, 1)
                        v.wait_ge(last_added, 2 * hf + 2)
                        half_stats(hf)

            with v.Fori(0, E0 // 2 - 1) as j:
                m0_body(j, False)
            m0_body(E0 // 2 - 1, True)

            def query_constants(hf):
                v.wait_ge(small_ev, 2)
                v.wait_ge(r_mm, hf + 1)
                v.tensor_tensor(rr[:], v3(bank[6][:, 0:HT * NH], NH),
                                att_small[:, 2 * NH:3 * NH].unsqueeze(1).broadcast_to([P, HT, NH]),
                                ALU.add).then_inc(r_ev, 1)
                v.wait_ge(r_ev, hf + 1)

            def less_maximum(hf, tp):
                m = 2 * hf + tp
                v.wait_ge(s_mm, m + 1)
                v.transpose(score_q[:, tp].rearrange("p n b -> p (n b)"), bank[2 + tp][:]).then_inc(s_ev, 1)
                v.wait_ge(s_ev, m + 1)
                step(v.tensor_reduce(row[:, 0], score_q[:, tp], AX.X, ALU.max))
                r = rr[:, 2 * tp:2 * tp + 2].rearrange("p i n -> p (i n)")
                step(v.tensor_tensor(row[:, 0], row[:, 0], r, ALU.add))
                step(v.tensor_tensor(row[:, 1], row[:, 0], r, ALU.subtract))
                v.tensor_tensor(score_q[:, tp], score_q[:, tp], row[:, 1].unsqueeze(2).broadcast_to([P, 2 * NH, BLK]),
                                ALU.subtract).then_inc(s_sub, 1)

            def probabilities(hf, tp):
                m = 2 * hf + tp
                v.wait_ge(s_exp, m + 1)
                step(v.tensor_reduce(row[:, 2], score_q[:, tp], AX.X, ALU.add))
                step(v.reciprocal(row[:, 3], row[:, 2]))
                step(v.tensor_tensor(score_q[:, tp], score_q[:, tp],
                                     row[:, 3].unsqueeze(2).broadcast_to([P, 2 * NH, BLK]), ALU.mult))
                if hf:
                    v.wait_ge(px_rdy, 4 * (tp + 1))
                v.transpose(pT[:, tp].rearrange("p n b -> p (n b)"),
                            score_q[:, tp].rearrange("p n b -> p (n b)")).then_inc(pt_rdy, 1)

            normalise(5, 1)
            low_part(5, 1)
            query_constants(0)
            less_maximum(0, 0)
            less_maximum(0, 1)
            probabilities(0, 0)
            probabilities(0, 1)
            query_constants(1)
            less_maximum(1, 0)
            less_maximum(1, 1)
            probabilities(1, 0)
            probabilities(1, 1)
            residual(0, [bank[6], bank[6]], av_mm, 2, av_hb, av_ev)
            normalise(6, 0)
            low_part(6, 0)
            residual(1, [bank[2], bank[6]], av_mm, 2, av_hb, av_ev)

            def gated(u, k, chunks=range(2)):
                for c in chunks:
                    q, r = 2 * u + c, (2 * k + c) % 3
                    v.wait_ge(silu_rdy, q + 1)
                    v.wait_ge(b_mm, q + 13)
                    if c == 0:
                        v.wait_ge(y1_mm, u + 1)
                    v.tensor_tensor(hid1[:, k % 2, c], sa[:, r], bank[3 + r][:], ALU.mult).then_inc(hid1_rdy, 1)

            def accumulate(u, e, k, last=False):
                hf = k % 2
                v.wait_ge(acc_rdy, u + 1)
                for i in range(HT):
                    if last and i == 0:
                        v.wait_ge(y1_two, 1)
                    elif i == (2 if last else 0):
                        v.wait_ge(y1_mm, u + 3)
                    ti = hf * HT + i
                    ins = v.scalar_tensor_tensor(h[:, ti], y1(k, i, last)[:, i * D:(i + 1) * D],
                                                 comb1[:, bass.ds(e, 1), ti:ti + 1].rearrange("p a i -> p (a i)"),
                                                 h[:, ti], ALU.mult, ALU.add)
                    if last and i == 1:
                        ins.then_inc(acc_two, 1)
                ins.then_inc(acc_rdy, 1)

            step(v.memset(comb1[:, 0], 1.0))
            gated(0, 0, [0])
            normalise(7, 1)
            gated(0, 0, [1])
            low_part(7, 1)
            v.wait_ge(gate_mm, 2)
            v.tensor_copy(lg[:], v3(bank[7][:, 0:NT * E0], E0)).then_inc(gate_ev, 1)
            v.wait_ge(gate_ev, 2)
            step(v.tensor_tensor(lgb[:], lg[:], m1_bias[:].unsqueeze(1).broadcast_to([P, NT, E0]), ALU.add))
            for i in range(NT):
                ins = v.max(top[:, i], lg[:, i])
            step(ins)
            v.tensor_copy(gwt[:], top[:, :, 0:2]).then_inc(gate_dif, 1)
            for i in range(NT):
                ins = v.max(topb[:, i], lgb[:, i])
            step(ins)
            for i in range(NT):
                ins = v.max_index(idx[:, i], topb[:, i], lgb[:, i])
            step(ins)
            gated(1, 1)
            v.wait_ge(gate_sig, 2)
            step(v.tensor_scalar(gw2[:], gw2[:], 1.0, None, ALU.add))
            step(v.reciprocal(gw2[:], gw2[:]))
            step(v.tensor_reduce(row[:, 0, 0:NT], gw2[:], AX.X, ALU.add))
            step(v.reciprocal(row[:, 1, 0:NT], row[:, 0, 0:NT]))
            step(v.tensor_tensor(gw2[:], gw2[:], row[:, 1, 0:NT].unsqueeze(2).broadcast_to([P, NT, 2]), ALU.mult))

            def write1(k):
                w = gw2[:, :, k:k + 1].broadcast_to([P, NT, E0])
                if k == 0:
                    step(v.tensor_tensor(lg[:], eq[:], w, ALU.mult))
                else:
                    step(v.tensor_tensor(eq[:], eq[:], w, ALU.mult))
                    step(v.tensor_tensor(comb1[:, 1:E1], lg[:].rearrange("p i e -> p e i"),
                                         eq[:].rearrange("p i e -> p e i"), ALU.add))

            one_hots(write1)

            def m1_body(j, tail):
                for k in range(M1_UNITS):
                    u = M1_UNITS * j + k
                    accumulate(u, 3 * j + k // 2, k, tail and k + 1 == M1_UNITS)
                    if not tail or k + 2 < M1_UNITS:
                        gated(u + 2, k + 2)

            with v.Fori(0, E1 // 3 - 1) as j:
                m1_body(j, False)
            m1_body(E1 // 3 - 1, True)


def kernel(**inputs):
    import numpy as np
    import concourse.bacc as bacc
    from concourse.bass_utils import run_bass_kernel_spmd

    a = {k: np.asarray(v) for k, v in inputs.items()}
    B = a["x"].shape[0]
    x = a["x"].reshape(B, 3, 4, 16, 4, 16).transpose(1, 3, 5, 0, 2, 4).reshape(KC, P, NT, P).transpose(2, 1, 0, 3)
    host = {
        "x": x,
        "tok_w": a["L0_tok_W"].T.reshape(KC, P, D).transpose(1, 0, 2),
        "tok_b": a["L0_tok_b"],
        "gru_w": a["L0_attn_W_in"].T,
        "gru_b": a["L0_attn_b_in"].reshape(4, P).T,
        "gru_wo": a["L0_attn_W_out"].T.reshape(HG, P, D).transpose(1, 0, 2),
        "gru_bo": a["L0_attn_b_out"],
        "wqT": a["L1_attn_Wq"].transpose(2, 0, 1),
        "wkT": a["L1_attn_Wk"].transpose(2, 0, 1),
        "wvT": a["L1_attn_Wv"].transpose(2, 0, 1),
        "wo": a["L1_attn_Wo"].reshape(NH, P, D).transpose(1, 0, 2),
        "att_b": np.stack([a["L1_attn_bq"], a["L1_attn_bk"], a["L1_attn_bv"]]).transpose(2, 0, 1),
        "m0_gate": a["L0_ffn_Wg"],
        "m0_w1": a["L0_ffn_W1"].transpose(1, 0, 2),
        "m0_b1": a["L0_ffn_b1"].T,
        "m0_w2": a["L0_ffn_W2"].transpose(1, 0, 2),
        "m0_b2": a["L0_ffn_b2"],
        "m0_gamma": a["L0_ffn_gamma"],
        "m0_beta": a["L0_ffn_beta"],
        "m1_gate": a["L1_ffn_gate_w"].T,
        "m1_bias": a["L1_ffn_biases"],
        "m1_w13": np.concatenate([np.concatenate([a["L1_ffn_sw1"][None], a["L1_ffn_w1"]]),
                                  np.concatenate([a["L1_ffn_sw3"][None], a["L1_ffn_w3"]])],
                                 axis=2).transpose(1, 0, 2).reshape(D, E1, 4, P),
        "m1_w2": np.concatenate([a["L1_ffn_sw2"][None], a["L1_ffn_w2"]]).reshape(E1, 2, P, D).transpose(2, 0, 1, 3),
    }
    nc = bacc.Bacc("TRN2", target_bir_lowering=False, num_devices=1)
    arrays, aps = {}, {}
    for name, value in host.items():
        arrays[f"in_{name}"] = np.ascontiguousarray(value)
        aps[name] = nc.dram_tensor(f"in_{name}", arrays[f"in_{name}"].shape, mybir.dt.float32, kind="ExternalInput").ap()
    out = nc.dram_tensor("out", (TOK, D), mybir.dt.float32, kind="ExternalOutput").ap()
    build(nc, aps, out)
    r = run_bass_kernel_spmd(nc, [arrays], core_ids=[0])
    return r.results[0]["out"].reshape(B, SEQ, D)
```
